# Optimizing a Trainium2 kernel written in Bass

```python
import numpy as np
import jax
import jax.numpy as jnp

def _softmax(x, axis=-1):
    return jax.nn.softmax(x, axis=axis)

def _gelu(x):
    return jax.nn.gelu(x, approximate=True)

def _silu(x):
    return jax.nn.silu(x)

def _sigmoid(x):
    return jax.nn.sigmoid(x)

def _layernorm(x, axis=-1, eps=1e-05):
    m = jnp.mean(x, axis=axis, keepdims=True)
    v = jnp.var(x, axis=axis, keepdims=True)
    return (x - m) / jnp.sqrt(v + eps)

def _scatter_add(tgt, idx, src, axis=0):
    return tgt.at[idx].add(src)

def _segment_sum(src, seg, n):
    return jax.ops.segment_sum(src, seg, n)
kernel_name = 'mk_gnn_resnorm_d1_gnn_r8_3a8f78'

def setup_inputs(seed: int=0):
    np.random.seed(seed)
    _w = jnp.asarray

    def _rec_inputs():
        import jax
        import jax.numpy as jnp
        _gk = jax.random.key(seed)
        x = -8.776e-05 + 1 * jax.random.normal(jax.random.fold_in(_gk, 1), (6250, 256), jnp.float32)
        _s = jax.random.randint(jax.random.fold_in(_gk, 2), (100000,), 0, 6250, jnp.int32)
        _d = jax.random.randint(jax.random.fold_in(_gk, 3), (100000,), 0, 6250, jnp.int32)
        _loop = jnp.arange(6250, dtype=jnp.int32)
        src = jnp.concatenate([_s, _d, _loop])
        dst = jnp.concatenate([_d, _s, _loop])
        _o = jnp.argsort(dst, stable=True)
        src = src[_o]
        dst = dst[_o]
        edge_type_16 = jax.random.randint(jax.random.fold_in(_gk, 12), (206250,), 0, 16, jnp.int32)
        edge_weight1 = jax.random.uniform(jax.random.fold_in(_gk, 13), (206250, 1), jnp.float32, 0.0, 0.999998)
        return (x, src, dst, edge_type_16, edge_weight1)
    x, src, dst, edge_type_16, edge_weight1 = _rec_inputs()

    def _L0_gnn_setup():
        import jax, jax.numpy as jnp
        import numpy as np
        N_NODES = 2500
        N_EDGES = 40000
        NUM_RELS = 16
        IN_FEAT = 256
        OUT_FEAT = 256
        key = jax.random.key(seed)
        k_h, k_w, k_n, k_s, k_d, k_r = jax.random.split(key, 6)
        h = jax.random.normal(k_h, (N_NODES, IN_FEAT), dtype=jnp.float32)
        weight = jax.random.normal(k_w, (NUM_RELS, IN_FEAT, OUT_FEAT), dtype=jnp.float32)
        norm = jax.random.uniform(k_n, (N_EDGES, 1), dtype=jnp.float32)
        src = jax.random.randint(k_s, (N_EDGES,), 0, N_NODES, dtype=jnp.int32)
        dst = jax.random.randint(k_d, (N_EDGES,), 0, N_NODES, dtype=jnp.int32)
        rel_type = jax.random.randint(k_r, (N_EDGES,), 0, NUM_RELS, dtype=jnp.int32)
        return {'h': h, 'weight': weight, 'norm': norm, 'src': src, 'dst': dst, 'rel_type': rel_type}
    _L0_gnn_all = _L0_gnn_setup()
    _L0_gnn_in = {k: v for k, v in _L0_gnn_all.items() if k in ('weight',)}
    del _L0_gnn_all
    return {'x': x, 'src': src, 'dst': dst, 'edge_type_16': edge_type_16, 'edge_weight1': edge_weight1, 'L0_gnn_weight': _L0_gnn_in['weight']}

def reference(x, src, dst, edge_type_16, edge_weight1, L0_gnn_weight):
    import jax
    import jax.numpy as jnp

    def _L0_gnn_ref(h, weight, norm, src, dst, rel_type):
        import jax, jax.numpy as jnp
        import numpy as np
        N_NODES = 2500
        N_EDGES = 40000
        NUM_RELS = 16
        IN_FEAT = 256
        OUT_FEAT = 256
        transformed = jnp.einsum('ni,rio->rno', h, weight)
        msg = transformed[rel_type, src] * norm
        out = jax.ops.segment_sum(msg, dst, num_segments=h.shape[0])
        return out
    x = _layernorm(x + _L0_gnn_ref(x, L0_gnn_weight, edge_weight1, src, dst, edge_type_16), axis=-1)
    return x

_drawn_inputs = setup_inputs


def setup_inputs(seed=0):
    import zlib

    import numpy as np

    out = dict(_drawn_inputs(seed))
    spreads = {}
    factors = {}
    for name, (base, spread) in spreads.items():
        noise = np.random.default_rng([zlib.crc32(name.encode()), seed]).standard_normal(out[name].shape)
        drawn = base * np.exp(spread * noise) if base else spread * noise
        out[name] = jnp.asarray(drawn.astype(out[name].dtype))
    for name, factor in factors.items():
        out[name] = (out[name] * factor).astype(out[name].dtype)
    return out
```

```python
from contextlib import ExitStack

import concourse.bass as bass
from concourse import mybir

ALU = mybir.AluOpType
ACT = mybir.ActivationFunctionType
F32 = mybir.dt.float32
I32 = mybir.dt.int32
P = 128
EPS = 1e-5


def build(nc, x, src, dst, rel, norm, weight, out):
    N, F = x.shape
    E = src.shape[0]
    R = weight.shape[0]
    KH = F // P
    ET = 125
    NT = E // ET
    NR = 125
    NN = N // NR
    assert NT * ET == E and NN * NR == N and KH * P == F

    acc = nc.dram_tensor("acc", [N, F], F32, kind="Internal").ap()

    with ExitStack() as ctx:
        def sb(name, shape, dt=F32):
            return ctx.enter_context(nc.sbuf_tensor(name, shape, dt))

        def sem(name):
            return ctx.enter_context(nc.semaphore(name))

        w_sb = sb("w_sb", [P, R, KH, F])
        ident = sb("ident", [P, P])
        earlier = sb("earlier", [P, P])
        rel_iota = sb("rel_iota", [P, R])
        eps_col = sb("eps_col", [P, 1])
        g_src = sb("g_src", [P, 1], I32)
        g_dst = sb("g_dst", [P, 1], I32)
        g_rel = sb("g_rel", [P, 1], I32)
        g_norm = sb("g_norm", [P, 1])
        g_dstf = sb("g_dstf", [P, 1])
        g_relf = sb("g_relf", [P, 1])
        g_dstw = sb("g_dstw", [P, P])
        g_rows = sb("g_rows", [P, F])
        g_cur = sb("g_cur", [P, F])
        g_msg = sb("g_msg", [P, F])
        g_msgT = sb("g_msgT", [P, KH, P])
        g_mask = sb("g_mask", [P, R])
        g_y = sb("g_y", [P, F])
        g_eq = sb("g_eq", [P, P])
        g_dup = sb("g_dup", [P, P])
        g_ndup = sb("g_ndup", [P, 1])
        g_to = sb("g_to", [P, 1])
        g_toi = sb("g_toi", [P, 1], I32)
        n_stat = sb("n_stat", [P, 6])
        n_mv = sb("n_mv", [P, 2])
        n_std = sb("n_std", [P, 1])
        n_rstd = sb("n_rstd", [P, 1])
        n_out = sb("n_out", [P, F])
        ps_t = ctx.enter_context(nc.psum_tensor("ps_t", [P, KH, P], F32))
        ps_d = ctx.enter_context(nc.psum_tensor("ps_d", [P, P], F32))
        ps_r = ctx.enter_context(nc.psum_tensor("ps_r", [P, 2, F * 2], F32))
        ps_s = ctx.enter_context(nc.psum_tensor("ps_s", [P, F], F32))

        s_w = sem("s_w")
        s_const = sem("s_const")
        s_acc = sem("s_acc")
        s_start = sem("s_start")
        s_meta = sem("s_meta")
        s_row = sem("s_row")
        s_cur = sem("s_cur")
        s_msg = sem("s_msg")
        s_tp = sem("s_tp")
        s_tc = sem("s_tc")
        s_rel = sem("s_rel")
        s_relu = sem("s_relu")
        s_sum = sem("s_sum")
        s_upd = sem("s_upd")
        s_store = sem("s_store")
        s_v = sem("s_v")
        s_nin = sem("s_nin")
        s_nstd = sem("s_nstd")
        s_nvar = sem("s_nvar")
        s_nout = sem("s_nout")
        s_nst = sem("s_nst")
        s_free = sem("s_free")
        s_tick = sem("s_tick")

        block = ctx.enter_context(nc.Block())
        G = slice(0, ET)

        @block.sync
        def _(sp):
            sp.dma_start(acc, x).then_inc(s_acc, 16)
            sp.dma_start(w_sb[:, :, :, :], weight.rearrange("r (k p) n -> p r k n", p=P)).then_inc(s_w, 16)
            sp.wait_ge(s_start, 1)
            sp.wait_ge(s_acc, 16)
            with sp.Fori(0, NT) as i:
                sp.wait_ge(s_free, i + 1)
                sp.sem_inc(s_tick, 1)
                at = bass.ds(i * ET, ET)
                sp.dma_start(g_src[G, :], src[at].rearrange("(p a) -> p a", a=1)).then_inc(s_meta, 16)
                sp.dma_start(g_dst[G, :], dst[at].rearrange("(p a) -> p a", a=1)).then_inc(s_meta, 16)
                sp.dma_start(g_rel[G, :], rel[at].rearrange("(p a) -> p a", a=1)).then_inc(s_meta, 16)
                sp.dma_start(g_norm[G, :], norm[at, :]).then_inc(s_meta, 16)
            sp.wait_ge(s_free, NT + 1)
            with sp.Fori(0, NN) as t:
                sp.dma_start(g_rows[0:NR, :], acc[bass.ds(t * NR, NR), :]).then_inc(s_nin, 16)
                sp.wait_ge(s_nout, t + 1)
                sp.sem_inc(s_tick, 1)
                sp.dma_start(out[bass.ds(t * NR, NR), :], n_out[0:NR, :]).then_inc(s_nst, 16)
                sp.wait_ge(s_nst, t * 16 + 16)
                sp.sem_inc(s_tick, 1)

        @block.gpsimd
        def _(pool):
            pool.memset(ident[:, :], 0.0).then_inc(s_const, 1)
            pool.memset(earlier[:, :], 1.0).then_inc(s_const, 1)
            pool.memset(eps_col[:, :], EPS).then_inc(s_const, 1)
            pool.iota(rel_iota[:, :], [[1, R]], base=0, channel_multiplier=0,
                      allow_small_or_imprecise_dtypes=True).then_inc(s_const, 1)
            pool.wait_ge(s_const, 4)
            pool.affine_select(out=ident[:, :], in_=ident[:, :], compare_op=ALU.not_equal, fill=1.0,
                               base=0, pattern=[[-1, P]], channel_multiplier=1).then_inc(s_const, 1)
            pool.affine_select(out=earlier[:, :], in_=earlier[:, :], compare_op=ALU.is_gt, fill=0.0,
                               base=0, pattern=[[-1, P]], channel_multiplier=1).then_inc(s_const, 1)
            pool.wait_ge(s_const, 6)
            pool.sem_inc(s_free, 1)
            pool.sem_inc(s_start, 1)
            pool.wait_ge(s_acc, 16)
            last_row = pool.to_reg(N - 1)
            with pool.Fori(0, NT) as i:
                pool.wait_ge(s_meta, i * 64 + 64)
                pool.sem_inc(s_tick, 1)
                pool.indirect_dma_start(g_rows[G, :], None, x, bass.IndirectOffsetOnAxis(ap=g_src[G, :], axis=0),
                                        bounds_check=last_row, oob_is_err=False).then_inc(s_row, 16)
                pool.indirect_dma_start(g_cur[G, :], None, acc, bass.IndirectOffsetOnAxis(ap=g_dst[G, :], axis=0),
                                        bounds_check=last_row, oob_is_err=False).then_inc(s_cur, 16)
                pool.wait_ge(s_upd, i + 1)
                pool.sem_inc(s_tick, 1)
                pool.indirect_dma_start(acc, bass.IndirectOffsetOnAxis(ap=g_toi[G, :], axis=0), g_cur[G, :], None,
                                        bounds_check=last_row, oob_is_err=False).then_inc(s_store, 16)
                pool.wait_ge(s_store, i * 16 + 16)
                pool.sem_inc(s_free, 1)

        @block.vector
        def _(dve):
            dve.wait_ge(s_const, 6)
            with dve.Fori(0, NT) as i:
                n = 0
                c = i * 11

                def done(ins):
                    ins.then_inc(s_v, 1)

                dve.wait_ge(s_meta, i * 64 + 64)
                done(dve.tensor_copy(g_dstf[G, :], g_dst[G, :]))
                done(dve.tensor_copy(g_relf[G, :], g_rel[G, :]))
                dve.wait_ge(s_v, c + 2)
                done(dve.tensor_scalar(g_mask[G, :], rel_iota[G, :], g_relf[G, :], None, ALU.is_equal))
                done(dve.tensor_scalar(g_dstw[G, 0:ET], ident[G, 0:ET], 0.0, g_dstf[G, :], ALU.mult, ALU.add))
                dve.wait_ge(s_row, i * 16 + 16)
                done(dve.tensor_scalar(g_msg[G, :], g_rows[G, :], g_norm[G, :], None, ALU.mult))
                dve.wait_ge(s_tp, i * 3 + 3)
                done(dve.tensor_scalar(g_eq[G, 0:ET], ps_d[G, 0:ET], g_dstf[G, :], None, ALU.is_equal))
                dve.wait_ge(s_v, c + 6)
                done(dve.tensor_tensor(g_dup[G, 0:ET], g_eq[G, 0:ET], earlier[G, 0:ET], ALU.mult))
                dve.wait_ge(s_v, c + 7)
                done(dve.reduce_sum(g_ndup[G, :], g_dup[G, 0:ET], axis=mybir.AxisListType.X))
                dve.wait_ge(s_v, c + 8)
                done(dve.scalar_tensor_tensor(out=g_to[G, :], in0=g_ndup[G, :], scalar=float(2 ** 16), in1=g_dstf[G, :],
                                              op0=ALU.mult, op1=ALU.add))
                dve.wait_ge(s_v, c + 9)
                done(dve.tensor_copy(g_toi[G, :], g_to[G, :]))
                for r in range(R):
                    dve.wait_ge(s_rel, i * R + r + 1)
                    if r == 0:
                        dve.tensor_scalar(g_y[G, :], ps_r[G, r % 2, 0:F], g_mask[G, r:r + 1], None,
                                          ALU.mult).then_inc(s_relu, 1)
                    else:
                        dve.wait_ge(s_relu, i * R + r)
                        dve.scalar_tensor_tensor(out=g_y[G, :], in0=ps_r[G, r % 2, 0:F], scalar=g_mask[G, r:r + 1],
                                                 in1=g_y[G, :], op0=ALU.mult, op1=ALU.add).then_inc(s_relu, 1)
                dve.wait_ge(s_sum, i + 1)
                dve.wait_ge(s_cur, i * 16 + 16)
                done(dve.tensor_tensor(g_cur[G, :], g_cur[G, :], ps_s[G, :], ALU.add))
                dve.wait_ge(s_v, c + 11)
                dve.sem_inc(s_upd, 1)
            L = slice(0, NR)
            with dve.Fori(0, NN) as t:
                dve.wait_ge(s_nin, t * 16 + 16)
                c = NT * 11 + t * 4
                dve.bn_stats(n_stat[L, :], g_rows[L, :]).then_inc(s_v, 1)
                dve.wait_ge(s_v, c + 1)
                dve.sem_inc(s_tick, 1)
                dve.bn_aggr(n_mv[L, :], n_stat[L, :]).then_inc(s_v, 1)
                dve.wait_ge(s_v, c + 2)
                dve.sem_inc(s_nvar, 1)
                dve.wait_ge(s_nstd, t + 1)
                dve.reciprocal(n_rstd[L, :], n_std[L, :]).then_inc(s_v, 1)
                dve.wait_ge(s_v, c + 3)
                dve.tensor_scalar(n_out[L, :], g_rows[L, :], n_mv[L, 0:1], n_rstd[L, :],
                                  ALU.subtract, ALU.mult).then_inc(s_v, 1)
                dve.wait_ge(s_v, c + 4)
                dve.sem_inc(s_nout, 1)

        @block.scalar
        def _(act):
            act.wait_ge(s_const, 6)
            with act.Fori(0, NT) as i:
                act.wait_ge(s_tp, i * 3 + 2)
                act.activation(g_msgT[:, :, 0:ET], ps_t[:, :, 0:ET], ACT.Copy).then_inc(s_tc, 1)
            with act.Fori(0, NN) as t:
                act.wait_ge(s_nvar, t + 1)
                act.activation(n_std[0:NR, :], n_mv[0:NR, 1:2], ACT.Sqrt, bias=eps_col[0:NR, :]).then_inc(s_nstd, 1)

        @block.tensor
        def _(pe):
            pe.wait_ge(s_w, 16)
            pe.wait_ge(s_const, 6)
            with pe.Fori(0, NT) as i:
                pe.wait_ge(s_v, i * 11 + 5)
                for k in range(KH):
                    pe.transpose(ps_t[:, k, 0:ET], g_msg[G, k * P:(k + 1) * P], ident[G, 0:ET]).then_inc(s_tp, 1)
                pe.transpose(ps_d[G, 0:ET], g_dstw[G, 0:ET], ident[G, 0:ET]).then_inc(s_tp, 1)
                pe.wait_ge(s_tc, i + 1)
                for r in range(R):
                    if r >= 2:
                        pe.wait_ge(s_relu, i * R + r - 1)
                    for k in range(KH):
                        ins = pe.matmul(ps_r[G, r % 2, 0:F], g_msgT[:, k, 0:ET], w_sb[:, r, k, :],
                                        start=k == 0, stop=k == KH - 1)
                    ins.then_inc(s_rel, 1)
                pe.wait_ge(s_relu, i * R + R)
                pe.matmul(ps_s[G, :], g_eq[G, 0:ET], g_y[G, :], start=True, stop=True).then_inc(s_sum, 1)


_INS = ["x", "src", "dst", "edge_type_16", "edge_weight1", "L0_gnn_weight"]


def kernel(**inputs):
    import numpy as np
    import concourse.bacc as bacc
    from concourse.bass_utils import run_bass_kernel_spmd

    nc = bacc.Bacc("TRN2", target_bir_lowering=False, num_devices=1)
    arrays, args = {}, []
    for name in _INS:
        a = np.ascontiguousarray(inputs[name])
        arrays[f"in_{name}"] = a
        args.append(nc.dram_tensor(f"in_{name}", a.shape, mybir.dt.from_np(a.dtype), kind="ExternalInput").ap())
    out = nc.dram_tensor("out", inputs["x"].shape, F32, kind="ExternalOutput").ap()
    build(nc, *args, out)
    return run_bass_kernel_spmd(nc, [arrays], core_ids=[0]).results[0]["out"]
```

```python
from contextlib import ExitStack
from math import ceil, sqrt

import concourse.bass as bass
from concourse import mybir

ALU = mybir.AluOpType
ACT = mybir.ActivationFunctionType
AX_X = mybir.AxisListType.X
F32 = mybir.dt.float32
F32R = mybir.dt.float32r
I32 = mybir.dt.int32
P = 128
EPS = 1e-5
SB = 128
UNIT = 4
SPREAD = 3.9


def windows(nodes, edges):
    degree = edges / nodes
    sigma = sqrt(degree)
    tiles = ceil((degree * SB + SPREAD * sigma * sqrt(SB)) / P)
    spans = []
    for b in range(0, SB, UNIT):
        first = degree * b - SPREAD * sigma * sqrt(b)
        last = degree * (b + UNIT) + SPREAD * sigma * sqrt(b + UNIT)
        spans.append((max(0, int(first // P)), min(tiles - 1, int(last // P))))
    found = []
    for t in range(tiles):
        units = [b for b, (first, last) in enumerate(spans) if first <= t <= last]
        found.append((UNIT * units[0], UNIT * (units[-1] + 1)))
    return found


def build(nc, x, src, dst, rel, norm, weight, out):
    N, F = x.shape
    E = src.shape[0]
    R = weight.shape[0]
    KH = F // P
    NB = ceil(N / SB)
    LAST = N - (NB - 1) * SB
    WIN = windows(N, E)
    CT = len(WIN)
    CE = CT * P
    WMAX = max(end - first for first, end in WIN) * R
    GN = 512 // R
    GROUPS = SB // GN
    OPEN = 2
    RING = 10
    BATCH = 7
    SROW = 330
    SROWS = E // SROW
    SP_ = 125
    SC = SROWS // SP_
    TAIL = 2 * CE
    PAD_DST = 1 << 19
    assert NB % 2 == 1 and 2 * CT % RING == 0 and CT % BATCH == 0 and GROUPS % OPEN == 0
    assert SROWS * SROW == E and SP_ * SC == SROWS and NB <= P and TAIL <= E

    group_tiles = []
    for g in range(GROUPS):
        hit = [t for t, (first, end) in enumerate(WIN) if first < (g + 1) * GN and end > g * GN]
        group_tiles.append((hit[0], hit[-1]))
    EVAC_LAG = 5
    META_SPLIT, META_COPY, META_KEYS = 1, 4, 6
    META_PE = 2
    PRODUCT_FROM = 4
    NORM_AT = 10
    products_after = []
    done_products = 0
    for t in range(CT):
        upto = 0 if t < PRODUCT_FROM else ceil(KH * R * (t - PRODUCT_FROM + 1) / (CT - PRODUCT_FROM))
        products_after.append(upto - done_products)
        done_products = upto

    ET = 125
    NT = E // ET
    NR = 125
    NN = N // NR
    assert NT * ET == E and NN * NR == N and KH * P == F and ET <= P

    acc = nc.dram_tensor("acc", [N, F], F32, kind="Internal").ap()
    tail = nc.dram_tensor("tail", [4, TAIL + CE], I32, kind="Internal").ap()
    norm_i = norm.rearrange("e a -> (e a)").bitcast(I32)

    with ExitStack() as ctx:
        def sb(name, shape, dt=F32):
            return ctx.enter_context(nc.sbuf_tensor(name, shape, dt))

        def sem(name):
            return ctx.enter_context(nc.semaphore(name))

        w_sb = sb("w_sb", [P, R, KH, F])
        ident = sb("ident", [P, P])
        earlier = sb("earlier", [P, P])
        rel_iota = sb("rel_iota", [P, R])
        eps_col = sb("eps_col", [P, 1])
        ones = sb("ones", [P, 1])
        bound_row = sb("bound_row", [P, NB])
        bound_col = sb("bound_col", [P, 1])
        sample_i = sb("sample_i", [P, SC], I32)
        sample = sb("sample", [P, SC])
        below = sb("below", [P, SC, NB])
        hit_row = sb("hit_row", [P, 1])
        hit_row_i = sb("hit_row_i", [P, 1], I32)
        hit_dst = sb("hit_dst", [P, SROW], I32)
        hit_cmp = sb("hit_cmp", [P, SROW])
        hit_cnt = sb("hit_cnt", [P, 1])
        first_edge = sb("first_edge", [P, 1])
        first_row = sb("first_row", [1, NB])
        first_i = sb("first_i", [1, NB], I32)
        pad_i = sb("pad_i", [64, 2, CE // 64], I32)
        raw = sb("raw", [CT, 4, P], I32)
        rawf = sb("rawf", [CT, 3, P])
        meta = sb("meta", [P, 2, 4, CT])
        idx = sb("idx", [P, 2, CT], I32)
        key_a = sb("key_a", [P, CT])
        key = sb("key", [P, 2, CT])
        key_in = sb("key_in", [P, CT])
        key_hit = sb("key_hit", [P, CT])
        hits = sb("hits", [P, 1])
        total = sb("total", [P, 1])
        win_base = sb("win_base", [P, CT])
        win_width = sb("win_width", [P, CT])
        block_base = sb("block_base", [P, NB + 1])
        col_iota = sb("col_iota", [P, WMAX])
        rows = sb("rows", [P, CT, F])
        hi = sb("hi", [P, RING, F], F32R)
        lo = sb("lo", [P, RING, F], F32R)
        onehot = sb("onehot", [P, RING, WMAX], F32R)
        a_sb = sb("a_sb", [P, 2, KH, R, SB])
        xr = sb("xr", [P, F])
        z = sb("z", [P, F])
        z_stat = sb("z_stat", [P, 6])
        z_mv = sb("z_mv", [P, 2])
        z_std = sb("z_std", [P, 1])
        z_rstd = sb("z_rstd", [P, 1])
        z_out = sb("z_out", [P, F])
        flag_f = sb("flag_f", [1, 1])
        flag_i = sb("flag_i", [1, 1], I32)
        g_src = sb("g_src", [P, 1], I32)
        g_dst = sb("g_dst", [P, 1], I32)
        g_rel = sb("g_rel", [P, 1], I32)
        g_norm = sb("g_norm", [P, 1])
        g_dstf = sb("g_dstf", [P, 1])
        g_relf = sb("g_relf", [P, 1])
        g_dstw = sb("g_dstw", [P, P])
        g_rows = sb("g_rows", [P, F])
        g_cur = sb("g_cur", [P, F])
        g_msg = sb("g_msg", [P, F])
        g_msgT = sb("g_msgT", [P, KH, P])
        g_mask = sb("g_mask", [P, R])
        g_y = sb("g_y", [P, F])
        g_eq = sb("g_eq", [P, P])
        g_dup = sb("g_dup", [P, P])
        g_ndup = sb("g_ndup", [P, 1])
        g_to = sb("g_to", [P, 1])
        g_toi = sb("g_toi", [P, 1], I32)
        n_stat = sb("n_stat", [P, 6])
        n_mv = sb("n_mv", [P, 2])
        n_std = sb("n_std", [P, 1])
        n_rstd = sb("n_rstd", [P, 1])
        n_out = sb("n_out", [P, F])

        ps_a = ctx.enter_context(nc.psum_tensor("ps_a", [P, OPEN, KH, GN * R], F32))
        ps_m = ctx.enter_context(nc.psum_tensor("ps_m", [P, 512], F32))
        ps_z = ctx.enter_context(nc.psum_tensor("ps_z", [P, 2, 512], F32))
        ps_t = ps_m[:, 0:KH * P].rearrange("p (k e) -> p k e", k=KH)
        ps_d = ps_z[:, 1, 0:P]
        ps_r = ps_a[:, :, 0, :]
        ps_s = ps_z[:, 0, 0:F]

        s_w = sem("s_w")
        s_const = sem("s_const")
        s_acc = sem("s_acc")
        s_start = sem("s_start")
        s_meta = sem("s_meta")
        s_row = sem("s_row")
        s_cur = sem("s_cur")
        s_msg = sem("s_msg")
        s_tp = sem("s_tp")
        s_tc = sem("s_tc")
        s_rel = sem("s_rel")
        s_relu = sem("s_relu")
        s_sum = sem("s_sum")
        s_upd = sem("s_upd")
        s_store = sem("s_store")
        s_v = sem("s_v")
        s_nin = sem("s_nin")
        s_nstd = sem("s_nstd")
        s_nvar = sem("s_nvar")
        s_nout = sem("s_nout")
        s_nst = sem("s_nst")
        s_free = sem("s_free")
        s_tick = sem("s_tick")

        s_ms = sem("s_ms")
        s_sample = sem("s_sample")
        s_pad = sem("s_pad")
        s_tail = sem("s_tail")
        s_padset = sem("s_padset")
        s_seek = sem("s_seek")
        s_seekt = sem("s_seekt")
        s_hitrow = sem("s_hitrow")
        s_hit = sem("s_hit")
        s_first = sem("s_first")
        s_firstt = sem("s_firstt")
        s_table = sem("s_table")
        s_raw = sem("s_raw")
        s_split = sem("s_split")
        s_rawt = sem("s_rawt")
        s_meta_f = sem("s_meta_f")
        s_keys = sem("s_keys")
        s_hi = sem("s_hi")
        s_lo = sem("s_lo")
        s_tile = sem("s_tile")
        s_evac = sem("s_evac")
        s_prod = sem("s_prod")
        s_xr = sem("s_xr")
        s_zadd = sem("s_zadd")
        s_zvar = sem("s_zvar")
        s_zstd = sem("s_zstd")
        s_z = sem("s_z")
        s_out = sem("s_out")
        s_f = sem("s_f")
        s_flag = sem("s_flag")
        s_total = sem("s_total")
        s_totalt = sem("s_totalt")
        s_go = sem("s_go")
        s_rows = [sem(f"s_rows{t}") for t in range(CT)]

        block = ctx.enter_context(nc.Block())
        G = slice(0, ET)

        def at(b, per, more):
            u, k = b
            return k * per + more if u is None else u * (2 * per) + (k * per + more)

        def wait(eng, s, b, per, more):
            if b[0] is None and at(b, per, more) <= 0:
                return
            eng.wait_ge(s, at(b, per, more))

        def blocks(eng, one):
            one((None, 0), True, False, False)
            one((None, 1), True, True, False)
            one((None, 2), True, True, True)
            with eng.Fori(1, (NB - 1) // 2) as u:
                one((u, 1), True, True, True)
                one((u, 2), True, True, True)
            one((None, NB), False, True, True)
            one((None, NB + 1), False, False, True)

        def ring_slot(b, t):
            return (b[1] * CT + t) % RING


        def fast_sync(sp):
            sp.dma_start(sample_i[0:SP_, :], dst.rearrange("(p c e) -> p c e", c=SC, e=SROW)[:, :, 0],
                         allow_slow_non_contiguous=True).then_inc(s_sample, 16)
            sp.dma_start(w_sb[:, :, :, :], weight.rearrange("r (k p) n -> p r k n", p=P)).then_inc(s_w, 16)
            for a, v in enumerate((src, dst, rel, norm_i)):
                sp.dma_start(tail[a, 0:TAIL].rearrange("(p e) -> p e", p=64),
                             v[E - TAIL:E].rearrange("(p e) -> p e", p=64)).then_inc(s_tail, 16)
            sp.wait_ge(s_padset, 2)
            for a in range(4):
                sp.dma_start(tail[a, TAIL:TAIL + CE].rearrange("(p e) -> p e", p=64),
                             pad_i[:, int(a == 1), :]).then_inc(s_tail, 16)

            def load_edges(b, first, arrays):
                if isinstance(b, int):
                    if b > 0:
                        sp.wait_ge(s_split, b)
                        sp.wait_ge(s_rawt, b)
                for a, v in enumerate(arrays):
                    sp.dma_start(raw[:, a, :], v[bass.ds(first, CE)].rearrange("(j p) -> j p", p=P)).then_inc(s_raw, 16)

            edges = (src, dst, rel, norm_i)
            tails = [tail[a, :] for a in range(4)]
            sp.wait_ge(s_table, 1)
            for b in range(3):
                load_edges(b, sp.value_load(first_i[0:1, b:b + 1], min_val=0, max_val=E - CE), edges)
                if b == 0:
                    sp.dma_start(xr[:, :], x[0:SB, :]).then_inc(s_xr, 16)
            with sp.Fori(1, NB - 3) as b:
                sp.wait_ge(s_split, b + 2)
                sp.wait_ge(s_rawt, b + 2)
                sp.sem_inc(s_tick, 1)
                load_edges(None, sp.value_load(first_i[0:1, bass.ds(b + 2, 1)], min_val=0, max_val=E - CE), edges)
                sp.wait_ge(s_z, b)
                sp.sem_inc(s_tick, 1)
                sp.dma_start(out[bass.ds(b * SB - SB, SB), :], z_out[:, :]).then_inc(s_out, 16)
                sp.dma_start(xr[:, :], x[bass.ds(b * SB, SB), :]).then_inc(s_xr, 16)
            for b in range(NB - 3, NB):
                if b == NB - 3:
                    sp.wait_ge(s_tail, 8 * 16)
                    load_edges(NB - 1, sp.value_load(first_i[0:1, NB - 1:NB], min_val=0, max_val=TAIL), tails)
                if b == NB - 2:
                    load_edges(NB, TAIL, tails)
                sp.wait_ge(s_z, b)
                rows_of = min(SB, N - b * SB)
                sp.dma_start(out[(b - 1) * SB:b * SB, :], z_out[:, :]).then_inc(s_out, 16)
                sp.dma_start(xr[0:rows_of, :], x[b * SB:b * SB + rows_of, :]).then_inc(s_xr, 16)
            sp.wait_ge(s_z, NB)
            sp.dma_start(out[(NB - 1) * SB:N, :], z_out[0:LAST, :]).then_inc(s_out, 16)
            sp.wait_ge(s_out, NB * 16)

        def fast_pool(pool):
            pool.memset(ident[:, :], 0.0).then_inc(s_const, 1)
            pool.iota(bound_row[:, :], [[SB, NB]], base=0, channel_multiplier=0,
                      allow_small_or_imprecise_dtypes=True).then_inc(s_const, 1)
            pool.iota(bound_col[:, :], [[0, 1]], base=0, channel_multiplier=SB,
                      allow_small_or_imprecise_dtypes=True).then_inc(s_const, 1)
            pool.wait_ge(s_const, 3)
            pool.affine_select(out=ident[:, :], in_=ident[:, :], compare_op=ALU.not_equal, fill=1.0,
                               base=0, pattern=[[-1, P]], channel_multiplier=1).then_inc(s_const, 1)
            pool.memset(pad_i[:, 0, :], 0).then_inc(s_padset, 1)
            pool.memset(pad_i[:, 1, :], PAD_DST).then_inc(s_padset, 1)
            pool.iota(block_base[:, :], [[SB * R, NB + 1]], base=0, channel_multiplier=0,
                      allow_small_or_imprecise_dtypes=True).then_inc(s_const, 1)
            pool.iota(col_iota[:, :], [[1, WMAX]], base=0, channel_multiplier=0,
                      allow_small_or_imprecise_dtypes=True).then_inc(s_const, 1)
            pool.memset(earlier[:, :], 1.0).then_inc(s_const, 1)
            pool.iota(rel_iota[:, :], [[1, R]], base=0, channel_multiplier=0,
                      allow_small_or_imprecise_dtypes=True).then_inc(s_const, 1)
            pool.wait_ge(s_const, 8)
            pool.affine_select(out=earlier[:, :], in_=earlier[:, :], compare_op=ALU.is_gt, fill=0.0,
                               base=0, pattern=[[-1, P]], channel_multiplier=1).then_inc(s_const, 1)
            pool.wait_ge(s_hitrow, 1)
            pool.indirect_dma_start(hit_dst[0:NB, :], None, dst.rearrange("(r e) -> r e", e=SROW),
                                    bass.IndirectOffsetOnAxis(ap=hit_row_i[0:NB, :], axis=0),
                                    bounds_check=SROWS - 1, oob_is_err=False).then_inc(s_hit, 16)
            last_row = pool.to_reg(N - 1)

            def gather_block(b, sums, products, rows_):
                if not sums:
                    return
                for t in range(CT):
                    if t == 0:
                        wait(pool, s_keys, b, 1, 1)
                    if t % BATCH == 0:
                        wait(pool, s_lo, b, 2 * CT, 2 * (t + BATCH - CT))
                        pool.sem_inc(s_tick, 1)
                    pool.indirect_dma_start(rows[:, t, :], None, x,
                                            bass.IndirectOffsetOnAxis(ap=idx[:, b[1] % 2, t:t + 1], axis=0),
                                            bounds_check=last_row, oob_is_err=False).then_inc(s_rows[t], 16)

            blocks(pool, gather_block)

        def fast_vector(dve):
            nf = [0]

            def done(ins):
                ins.then_inc(s_f, 1)
                nf[0] += 1
                dve.wait_ge(s_f, nf[0])

            for t, (first, end) in enumerate(WIN):
                dve.memset(win_base[:, t:t + 1], float(first * R)).then_inc(s_ms, 1)
                dve.memset(win_width[:, t:t + 1], float((end - first) * R)).then_inc(s_ms, 1)
            dve.memset(ones[:, :], 1.0).then_inc(s_ms, 1)
            dve.memset(total[:, :], 0.0).then_inc(s_ms, 1)
            dve.memset(eps_col[:, :], EPS).then_inc(s_ms, 1)
            dve.wait_ge(s_const, 3)
            dve.wait_ge(s_sample, 16)
            done(dve.tensor_copy(sample[0:SP_, :], sample_i[0:SP_, :]))
            for c in range(SC):
                dve.tensor_scalar(below[0:SP_, c, :], bound_row[0:SP_, :], sample[0:SP_, c:c + 1], None,
                                  ALU.is_gt).then_inc(s_seek, 1)
            dve.wait_ge(s_seekt, 1)
            B = slice(0, NB)
            done(dve.tensor_scalar(hit_row[B, :], ps_m[B, 0:1], -1.0, 0.0, ALU.add, ALU.max))
            dve.tensor_copy(hit_row_i[B, :], hit_row[B, :]).then_inc(s_hitrow, 1)
            dve.wait_ge(s_hit, 16)
            done(dve.tensor_scalar(hit_cmp[B, :], hit_dst[B, :], bound_col[B, :], None, ALU.is_lt))
            done(dve.reduce_sum(hit_cnt[B, :], hit_cmp[B, :], axis=AX_X))
            dve.scalar_tensor_tensor(out=first_edge[B, :], in0=hit_row[B, :], scalar=float(SROW), in1=hit_cnt[B, :],
                                     op0=ALU.mult, op1=ALU.add).then_inc(s_first, 1)
            dve.wait_ge(s_firstt, 1)
            done(dve.tensor_scalar(first_row[0:1, 0:NB - 1], ps_m[0:1, 64:64 + NB - 1], float(E - CE), None, ALU.min))
            done(dve.tensor_scalar(first_row[0:1, NB - 1:NB], ps_m[0:1, 64 + NB - 1:64 + NB], float(-(E - TAIL)), 0.0,
                                   ALU.add, ALU.max))
            dve.tensor_copy(first_i[0:1, :], first_row[0:1, :]).then_inc(s_table, 1)

            def split_edges(b):
                wait(dve, s_raw, b, 64, 64)
                wait(dve, s_rawt, b, 1, 0)
                dve.tensor_copy(rawf[:, :, :], raw[:, 0:3, :]).then_inc(s_split, 1)

            def keys(b):
                k = b[1] % 2
                wait(dve, s_meta_f, b, 1, 1)
                m = meta[:, k, :, :]
                dve.tensor_copy(idx[:, k, :], m[:, 0, :]).then_inc(s_f, 1)
                dve.scalar_tensor_tensor(out=key_a[:, :], in0=m[:, 1, :], scalar=float(R), in1=m[:, 2, :],
                                         op0=ALU.mult, op1=ALU.add).then_inc(s_f, 1)
                wait(dve, s_f, b, 6, nf[0] + 2)
                base = block_base[:, b[1]:b[1] + 1] if b[0] is None else block_base[:, bass.ds(b[0] * 2 + b[1], 1)]
                dve.scalar_tensor_tensor(out=key[:, k, :], in0=key_a[:, :], scalar=base, in1=win_base[:, :],
                                         op0=ALU.subtract, op1=ALU.subtract).then_inc(s_f, 1)
                wait(dve, s_f, b, 6, nf[0] + 3)
                dve.sem_inc(s_keys, 1)
                dve.tensor_tensor(key_in[:, :], key[:, k, :], win_width[:, :], ALU.is_lt).then_inc(s_f, 1)
                wait(dve, s_f, b, 6, nf[0] + 4)
                dve.scalar_tensor_tensor(out=key_hit[:, :], in0=key[:, k, :], scalar=0.0, in1=key_in[:, :],
                                         op0=ALU.is_ge, op1=ALU.mult).then_inc(s_f, 1)
                wait(dve, s_f, b, 6, nf[0] + 5)
                dve.reduce_sum(hits[:, :], key_hit[:, :], axis=AX_X).then_inc(s_f, 1)
                wait(dve, s_f, b, 6, nf[0] + 6)
                dve.tensor_tensor(total[:, :], total[:, :], hits[:, :], ALU.add).then_inc(s_total, 1)

            def normalise(b):
                wait(dve, s_prod, b, 1, -1)
                wait(dve, s_xr, b, 16, -16)
                dve.tensor_tensor(z[:, :], xr[:, :], ps_z[:, b[1] % 2, 0:F], ALU.add).then_inc(s_zadd, 1)
                wait(dve, s_zadd, b, 1, -1)
                dve.bn_stats(z_stat[:, :], z[:, :]).then_inc(s_zvar, 1)
                wait(dve, s_zvar, b, 2, -3)
                dve.sem_inc(s_tick, 1)
                dve.bn_aggr(z_mv[:, :], z_stat[:, :]).then_inc(s_zvar, 1)
                wait(dve, s_zstd, b, 1, -1)
                dve.reciprocal(z_rstd[:, :], z_std[:, :]).then_inc(s_go, 1)
                wait(dve, s_go, b, 1, -1)
                wait(dve, s_out, b, 16, -32)
                dve.tensor_scalar(z_out[:, :], z[:, :], z_mv[:, 0:1], z_rstd[:, :],
                                  ALU.subtract, ALU.mult).then_inc(s_z, 1)

            def tile_block(b, sums, products, rows_):
                for t in range(CT):
                    if sums:
                        slot = ring_slot(b, t)
                        if t == META_SPLIT:
                            next_edges(split_edges, b)
                        if t == META_KEYS:
                            next_edges(keys, b)
                        first, end = WIN[t]
                        wait(dve, s_tile, b, CT, t + 1 - RING)
                        dve.tensor_scalar(onehot[:, slot, 0:(end - first) * R], col_iota[:, 0:(end - first) * R],
                                          key[:, b[1] % 2, t:t + 1], None, ALU.is_equal).then_inc(s_lo, 1)
                        wait(dve, s_hi, b, CT, t + 1)
                        dve.scalar_tensor_tensor(out=lo[:, slot, :], in0=rows[:, t, :], scalar=meta[:, b[1] % 2, 3, t:t + 1],
                                                 in1=hi[:, slot, :].bitcast(F32), op0=ALU.mult,
                                                 op1=ALU.subtract).then_inc(s_lo, 1)
                    if rows_ and t == NORM_AT:
                        normalise(b)

            split_edges((None, 0))
            keys((None, 0))
            dve.wait_ge(s_ms, 2 * CT + 3)
            dve.wait_ge(s_const, 6)
            blocks(dve, tile_block)
            dve.wait_ge(s_total, NB + 1)
            dve.sem_inc(s_totalt, 1)
            dve.wait_ge(s_flag, 1)
            done_total = dve.tensor_scalar(flag_f[:, :], ps_m[0:1, 256:257], float(E), None, ALU.not_equal)
            done_total.then_inc(s_flag, 1)
            dve.wait_ge(s_flag, 2)
            dve.tensor_copy(flag_i[:, :], flag_f[:, :]).then_inc(s_flag, 1)

        def next_edges(step, b):
            step((b[0], b[1] + 1))

        def fast_scalar(act):
            def copy_edges(b):
                k = b[1] % 2
                wait(act, s_rawt, b, 1, 1)
                wait(act, s_lo, b, 2 * CT, -2 * CT)
                act.activation(meta[:, k, :, :], ps_m[:, 0:4 * CT].rearrange("p (a t) -> p a t", a=4),
                               ACT.Copy).then_inc(s_meta_f, 1)

            def evacuate(b, g):
                wait(act, s_tile, b, CT, group_tiles[g][1] + 1)
                if g == 0:
                    wait(act, s_prod, b, 1, -1)
                for h in range(KH):
                    act.activation(a_sb[:, b[1] % 2, h, :, g * GN:(g + 1) * GN],
                                   ps_a[:, g % OPEN, h, :].rearrange("p (n r) -> p r n", r=R),
                                   ACT.Copy).then_inc(s_evac, 1)

            def tile_block(b, sums, products, rows_):
                for t in range(CT):
                    if sums:
                        if t == META_COPY:
                            next_edges(copy_edges, b)
                        slot = ring_slot(b, t)
                        wait(act, s_rows[t], b, 16, 16)
                        wait(act, s_tile, b, CT, t + 1 - RING)
                        if t == 0:
                            wait(act, s_meta_f, b, 1, 1)
                        act.activation(hi[:, slot, :], rows[:, t, :], ACT.Copy,
                                       scale=meta[:, b[1] % 2, 3, t:t + 1]).then_inc(s_hi, 1)
                    for g in range(GROUPS):
                        due = group_tiles[g][1] + EVAC_LAG
                        if sums and t == due:
                            evacuate(b, g)
                        if products and t == due - CT:
                            evacuate((b[0], b[1] - 1), g)
                    if rows_ and t == NORM_AT:
                        wait(act, s_zvar, b, 2, -2)
                        act.activation(z_std[:, :], z_mv[:, 1:2], ACT.Sqrt, bias=eps_col[:, :]).then_inc(s_zstd, 1)

            copy_edges((None, 0))
            blocks(act, tile_block)

        def fast_tensor(pe):
            pe.wait_ge(s_const, 4)
            pe.wait_ge(s_ms, 2 * CT + 3)
            pe.wait_ge(s_seek, SC)
            for c in range(SC):
                ins = pe.matmul(ps_m[0:NB, 0:1], below[0:SP_, c, :], ones[0:SP_, :], start=c == 0, stop=c == SC - 1)
            ins.then_inc(s_seekt, 1)
            pe.wait_ge(s_first, 1)
            pe.transpose(ps_m[0:1, 64:64 + NB], first_edge[0:NB, :], ident[0:NB, 0:NB]).then_inc(s_firstt, 1)

            def turn_edges(b):
                wait(pe, s_split, b, 1, 1)
                wait(pe, s_meta_f, b, 1, 0)
                pe.sem_inc(s_tick, 1)
                for a in range(4):
                    v = rawf[:, a, :] if a < 3 else raw[:, a, :].bitcast(F32)
                    ins = pe.transpose(ps_m[:, a * CT:(a + 1) * CT], v, ident[0:CT, 0:CT])
                ins.then_inc(s_rawt, 1)

            def product(b, n):
                r, h = n // KH, n % KH
                if n == 0:
                    wait(pe, s_evac, b, GROUPS * KH, 0)
                    wait(pe, s_zadd, b, 1, -2)
                ins = pe.matmul(ps_z[:, (b[1] + 1) % 2, 0:F], a_sb[:, (b[1] + 1) % 2, h, r, :], w_sb[:, r, h, :],
                                start=n == 0, stop=n == KH * R - 1)
                if n == KH * R - 1:
                    ins.then_inc(s_prod, 1)

            def tile_block(b, sums, products, rows_):
                n = 0
                for t in range(CT):
                    if sums:
                        slot = ring_slot(b, t)
                        if t == META_PE:
                            next_edges(turn_edges, b)
                        wait(pe, s_lo, b, 2 * CT, 2 * t + 2)
                        first, end = WIN[t]
                        groups = [g for g in range(GROUPS) if first < (g + 1) * GN and end > g * GN]
                        for g in groups:
                            if group_tiles[g][0] == t:
                                wait(pe, s_evac, b, GROUPS * KH, KH * (g + 1 - OPEN))
                        for h in range(KH):
                            for part in (hi, lo):
                                for g in groups:
                                    begin, stop = max(first, g * GN), min(end, (g + 1) * GN)
                                    opens = group_tiles[g][0] == t and part is hi
                                    ins = pe.matmul(
                                        ps_a[:, g % OPEN, h, (begin - g * GN) * R:(stop - g * GN) * R],
                                        part[:, slot, h * P:(h + 1) * P],
                                        onehot[:, slot, (begin - first) * R:(stop - first) * R],
                                        start=opens, stop=False, skip_group_check=True)
                        ins.then_inc(s_tile, 1)
                    if products:
                        for _ in range(products_after[t]):
                            product(b, n)
                            n += 1

            pe.wait_ge(s_table, 1)
            turn_edges((None, 0))
            pe.wait_ge(s_w, 16)
            blocks(pe, tile_block)
            pe.wait_ge(s_totalt, 1)
            pe.matmul(ps_m[0:1, 256:257], total[:, :], ones[:, :], start=True, stop=True).then_inc(s_flag, 1)

        def uncounted(eng):
            eng.wait_ge(s_flag, 3)
            return eng.value_load(flag_i[0:1, 0:1], min_val=0, max_val=1)


        def general_sync(sp):
            sp.dma_start(acc, x).then_inc(s_acc, 16)
            sp.wait_ge(s_start, 1)
            sp.wait_ge(s_acc, 16)
            with sp.Fori(0, NT) as i:
                sp.wait_ge(s_free, i + 1)
                sp.sem_inc(s_tick, 1)
                at = bass.ds(i * ET, ET)
                sp.dma_start(g_src[G, :], src[at].rearrange("(p a) -> p a", a=1)).then_inc(s_meta, 16)
                sp.dma_start(g_dst[G, :], dst[at].rearrange("(p a) -> p a", a=1)).then_inc(s_meta, 16)
                sp.dma_start(g_rel[G, :], rel[at].rearrange("(p a) -> p a", a=1)).then_inc(s_meta, 16)
                sp.dma_start(g_norm[G, :], norm[at, :]).then_inc(s_meta, 16)
            sp.wait_ge(s_free, NT + 1)
            with sp.Fori(0, NN) as t:
                sp.dma_start(g_rows[0:NR, :], acc[bass.ds(t * NR, NR), :]).then_inc(s_nin, 16)
                sp.wait_ge(s_nout, t + 1)
                sp.sem_inc(s_tick, 1)
                sp.dma_start(out[bass.ds(t * NR, NR), :], n_out[0:NR, :]).then_inc(s_nst, 16)
                sp.wait_ge(s_nst, t * 16 + 16)
                sp.sem_inc(s_tick, 1)

        def general_pool(pool):
            pool.sem_inc(s_free, 1)
            pool.sem_inc(s_start, 1)
            pool.wait_ge(s_acc, 16)
            last_row = pool.to_reg(N - 1)
            with pool.Fori(0, NT) as i:
                pool.wait_ge(s_meta, i * 64 + 64)
                pool.sem_inc(s_tick, 1)
                pool.indirect_dma_start(g_rows[G, :], None, x, bass.IndirectOffsetOnAxis(ap=g_src[G, :], axis=0),
                                        bounds_check=last_row, oob_is_err=False).then_inc(s_row, 16)
                pool.indirect_dma_start(g_cur[G, :], None, acc, bass.IndirectOffsetOnAxis(ap=g_dst[G, :], axis=0),
                                        bounds_check=last_row, oob_is_err=False).then_inc(s_cur, 16)
                pool.wait_ge(s_upd, i + 1)
                pool.sem_inc(s_tick, 1)
                pool.indirect_dma_start(acc, bass.IndirectOffsetOnAxis(ap=g_toi[G, :], axis=0), g_cur[G, :], None,
                                        bounds_check=last_row, oob_is_err=False).then_inc(s_store, 16)
                pool.wait_ge(s_store, i * 16 + 16)
                pool.sem_inc(s_free, 1)

        def general_vector(dve):
            dve.wait_ge(s_const, 9)
            with dve.Fori(0, NT) as i:
                n = 0
                c = i * 11

                def done(ins):
                    ins.then_inc(s_v, 1)

                dve.wait_ge(s_meta, i * 64 + 64)
                done(dve.tensor_copy(g_dstf[G, :], g_dst[G, :]))
                done(dve.tensor_copy(g_relf[G, :], g_rel[G, :]))
                dve.wait_ge(s_v, c + 2)
                done(dve.tensor_scalar(g_mask[G, :], rel_iota[G, :], g_relf[G, :], None, ALU.is_equal))
                done(dve.tensor_scalar(g_dstw[G, 0:ET], ident[G, 0:ET], 0.0, g_dstf[G, :], ALU.mult, ALU.add))
                dve.wait_ge(s_row, i * 16 + 16)
                done(dve.tensor_scalar(g_msg[G, :], g_rows[G, :], g_norm[G, :], None, ALU.mult))
                dve.wait_ge(s_tp, i * 3 + 3)
                done(dve.tensor_scalar(g_eq[G, 0:ET], ps_d[G, 0:ET], g_dstf[G, :], None, ALU.is_equal))
                dve.wait_ge(s_v, c + 6)
                done(dve.tensor_tensor(g_dup[G, 0:ET], g_eq[G, 0:ET], earlier[G, 0:ET], ALU.mult))
                dve.wait_ge(s_v, c + 7)
                done(dve.reduce_sum(g_ndup[G, :], g_dup[G, 0:ET], axis=mybir.AxisListType.X))
                dve.wait_ge(s_v, c + 8)
                done(dve.scalar_tensor_tensor(out=g_to[G, :], in0=g_ndup[G, :], scalar=float(2 ** 16), in1=g_dstf[G, :],
                                              op0=ALU.mult, op1=ALU.add))
                dve.wait_ge(s_v, c + 9)
                done(dve.tensor_copy(g_toi[G, :], g_to[G, :]))
                for r in range(R):
                    dve.wait_ge(s_rel, i * R + r + 1)
                    if r == 0:
                        dve.tensor_scalar(g_y[G, :], ps_r[G, r % 2, 0:F], g_mask[G, r:r + 1], None,
                                          ALU.mult).then_inc(s_relu, 1)
                    else:
                        dve.wait_ge(s_relu, i * R + r)
                        dve.scalar_tensor_tensor(out=g_y[G, :], in0=ps_r[G, r % 2, 0:F], scalar=g_mask[G, r:r + 1],
                                                 in1=g_y[G, :], op0=ALU.mult, op1=ALU.add).then_inc(s_relu, 1)
                dve.wait_ge(s_sum, i + 1)
                dve.wait_ge(s_cur, i * 16 + 16)
                done(dve.tensor_tensor(g_cur[G, :], g_cur[G, :], ps_s[G, :], ALU.add))
                dve.wait_ge(s_v, c + 11)
                dve.sem_inc(s_upd, 1)
            L = slice(0, NR)
            with dve.Fori(0, NN) as t:
                dve.wait_ge(s_nin, t * 16 + 16)
                c = NT * 11 + t * 4
                dve.bn_stats(n_stat[L, :], g_rows[L, :]).then_inc(s_v, 1)
                dve.wait_ge(s_v, c + 1)
                dve.sem_inc(s_tick, 1)
                dve.bn_aggr(n_mv[L, :], n_stat[L, :]).then_inc(s_v, 1)
                dve.wait_ge(s_v, c + 2)
                dve.sem_inc(s_nvar, 1)
                dve.wait_ge(s_nstd, t + 1)
                dve.reciprocal(n_rstd[L, :], n_std[L, :]).then_inc(s_v, 1)
                dve.wait_ge(s_v, c + 3)
                dve.tensor_scalar(n_out[L, :], g_rows[L, :], n_mv[L, 0:1], n_rstd[L, :],
                                  ALU.subtract, ALU.mult).then_inc(s_v, 1)
                dve.wait_ge(s_v, c + 4)
                dve.sem_inc(s_nout, 1)

        def general_scalar(act):
            with act.Fori(0, NT) as i:
                act.wait_ge(s_tp, i * 3 + 2)
                act.activation(g_msgT[:, :, 0:ET], ps_t[:, :, 0:ET], ACT.Copy).then_inc(s_tc, 1)
            with act.Fori(0, NN) as t:
                act.wait_ge(s_nvar, t + 1)
                act.activation(n_std[0:NR, :], n_mv[0:NR, 1:2], ACT.Sqrt, bias=eps_col[0:NR, :]).then_inc(s_nstd, 1)

        def general_tensor(pe):
            with pe.Fori(0, NT) as i:
                pe.wait_ge(s_v, i * 11 + 5)
                for k in range(KH):
                    pe.transpose(ps_t[:, k, 0:ET], g_msg[G, k * P:(k + 1) * P], ident[G, 0:ET]).then_inc(s_tp, 1)
                pe.transpose(ps_d[G, 0:ET], g_dstw[G, 0:ET], ident[G, 0:ET]).then_inc(s_tp, 1)
                pe.wait_ge(s_tc, i + 1)
                for r in range(R):
                    if r >= 2:
                        pe.wait_ge(s_relu, i * R + r - 1)
                    for k in range(KH):
                        ins = pe.matmul(ps_r[G, r % 2, 0:F], g_msgT[:, k, 0:ET], w_sb[:, r, k, :],
                                        start=k == 0, stop=k == KH - 1)
                    ins.then_inc(s_rel, 1)
                pe.wait_ge(s_relu, i * R + R)
                pe.matmul(ps_s[G, :], g_eq[G, 0:ET], g_y[G, :], start=True, stop=True).then_inc(s_sum, 1)

        @block.sync
        def _(sp):
            fast_sync(sp)
            with sp.If(uncounted(sp) == 1):
                general_sync(sp)

        @block.gpsimd
        def _(pool):
            fast_pool(pool)
            with pool.If(uncounted(pool) == 1):
                general_pool(pool)

        @block.vector
        def _(dve):
            fast_vector(dve)
            with dve.If(uncounted(dve) == 1):
                general_vector(dve)

        @block.scalar
        def _(act):
            fast_scalar(act)
            with act.If(uncounted(act) == 1):
                general_scalar(act)

        @block.tensor
        def _(pe):
            fast_tensor(pe)
            with pe.If(uncounted(pe) == 1):
                general_tensor(pe)


_INS = ["x", "src", "dst", "edge_type_16", "edge_weight1", "L0_gnn_weight"]


def kernel(**inputs):
    import numpy as np
    import concourse.bacc as bacc
    from concourse.bass_utils import run_bass_kernel_spmd

    nc = bacc.Bacc("TRN2", target_bir_lowering=False, num_devices=1)
    arrays, args = {}, []
    for name in _INS:
        a = np.ascontiguousarray(inputs[name])
        arrays[f"in_{name}"] = a
        args.append(nc.dram_tensor(f"in_{name}", a.shape, mybir.dt.from_np(a.dtype), kind="ExternalInput").ap())
    out = nc.dram_tensor("out", inputs["x"].shape, F32, kind="ExternalOutput").ap()
    build(nc, *args, out)
    return run_bass_kernel_spmd(nc, [arrays], core_ids=[0]).results[0]["out"]
```

```python
from contextlib import ExitStack
from itertools import count
from math import ceil, sqrt

import concourse.bass as bass
from concourse import mybir

ALU = mybir.AluOpType
ACT = mybir.ActivationFunctionType
AX_X = mybir.AxisListType.X
F32 = mybir.dt.float32
F32R = mybir.dt.float32r
I32 = mybir.dt.int32
P = 128
EPS = 1e-5
SB = 128
UNIT = 4
SPREAD = 3.9


def windows(nodes, edges):
    degree = edges / nodes
    sigma = sqrt(degree)
    tiles = ceil((degree * SB + SPREAD * sigma * sqrt(SB)) / P)
    spans = []
    for b in range(0, SB, UNIT):
        first = degree * b - SPREAD * sigma * sqrt(b)
        last = degree * (b + UNIT) + SPREAD * sigma * sqrt(b + UNIT)
        spans.append((max(0, int(first // P)), min(tiles - 1, int(last // P))))
    found = []
    for t in range(tiles):
        units = [b for b, (first, last) in enumerate(spans) if first <= t <= last]
        found.append((UNIT * units[0], UNIT * (units[-1] + 1)))
    return found


def build(nc, x, src, dst, rel, norm, weight, out):
    N, F = x.shape
    E = src.shape[0]
    R = weight.shape[0]
    KH = F // P
    NB = ceil(N / SB)
    LAST = N - (NB - 1) * SB
    WIN = windows(N, E)
    CT = len(WIN)
    CE = CT * P
    WMAX = max(end - first for first, end in WIN) * R
    GN = 512 // R
    GROUPS = SB // GN
    OPEN = 2
    RING = 10
    ROWS = 14
    BATCH = 5
    SROW = 330
    SROWS = E // SROW
    SP = 125
    SC = SROWS // SP
    TAIL = 2 * CE
    FIRST_AT, TOTAL_AT, HITS_AT = 64, 256, 300
    PAD_DST = 1 << 19
    assert NB % 2 == 1 and 2 * CT % RING == 0 and 2 * CT % ROWS == 0
    assert ROWS >= 2 * BATCH and CT % BATCH == 0 and GROUPS % OPEN == 0
    assert SROWS * SROW == E and SP * SC == SROWS and NB <= P and TAIL <= E

    group_tiles = []
    for g in range(GROUPS):
        hit = [t for t, (first, end) in enumerate(WIN) if first < (g + 1) * GN and end > g * GN]
        group_tiles.append((hit[0], hit[-1]))
    EVAC_LAG = 4
    PREPARE = (1, 2, 4, 6, 8, 12)
    PREPARE_0 = tuple(t + 19 for t in PREPARE)
    SEEK_ROW, SEEK_GATHER, SEEK_EDGE, SEEK_TURN, SEEK_TABLE = 2, 5, 10, 11, 13
    WEIGHTS_AT = {2 * n + 1: n for n in range(R)}
    WEIGHTS_BEFORE = 7
    OPTIONAL = (CT - 2, CT - 1)
    CONFIRM = 3
    PRODUCT_FROM = 4
    NORM_AT = 10
    products_after = []
    done_products = 0
    for t in range(CT):
        upto = 0 if t < PRODUCT_FROM else ceil(KH * R * (t - PRODUCT_FROM + 1) / (CT - PRODUCT_FROM))
        products_after.append(upto - done_products)
        done_products = upto

    ET = 125
    NT = E // ET
    NR = 125
    NN = N // NR
    assert NT * ET == E and NN * NR == N and KH * P == F and ET <= P

    acc = nc.dram_tensor("acc", [N, F], F32, kind="Internal").ap()
    tail = nc.dram_tensor("tail", [4, TAIL + CE], I32, kind="Internal").ap()
    norm_i = norm.rearrange("e a -> (e a)").bitcast(I32)

    with ExitStack() as ctx:
        def sb(name, shape, dt=F32):
            return ctx.enter_context(nc.sbuf_tensor(name, shape, dt))

        fast = ExitStack()

        def sbf(name, shape, dt=F32):
            return fast.enter_context(nc.sbuf_tensor(name, shape, dt))

        def sem(name):
            return ctx.enter_context(nc.semaphore(name))

        ident = sb("ident", [P, P])
        earlier = sb("earlier", [P, P])
        rel_iota = sb("rel_iota", [P, R])
        eps_col = sb("eps_col", [P, 1])
        ones = sb("ones", [P, 1])
        bound_row = sb("bound_row", [P, NB])
        bound_col = sb("bound_col", [P, 1])
        sample_i = sb("sample_i", [P, SC], I32)
        sample = sb("sample", [P, SC])
        below = sb("below", [P, SC, NB])
        hit_row = sb("hit_row", [P, 1])
        hit_row_i = sb("hit_row_i", [P, 1], I32)
        hit_dst = sb("hit_dst", [P, SROW], I32)
        hit_cmp = sb("hit_cmp", [P, SROW])
        hit_cnt = sb("hit_cnt", [P, 1])
        first_edge = sb("first_edge", [P, 1])
        first_row = sb("first_row", [1, NB])
        first_i = sb("first_i", [1, NB], I32)
        pad_i = sb("pad_i", [64, 2, CE // 64], I32)
        raw = sb("raw", [CT, 4, P], I32)
        raw_f = sb("raw_f", [CT, 3, P])
        meta = sb("meta", [P, 2, 4, CT])
        idx = sb("idx", [P, 2, CT], I32)
        key_a = sb("key_a", [P, CT])
        key = sb("key", [P, 2, CT])
        key_in = sb("key_in", [P, CT])
        key_hit = sb("key_hit", [P, CT])
        late_hits = sb("late_hits", [1, 2, len(OPTIONAL)], I32)
        hits = sb("hits", [P, 1])
        total = sb("total", [P, 1])
        win_base = sb("win_base", [P, CT])
        win_width = sb("win_width", [P, CT])
        block_base = sb("block_base", [P, NB + 1])
        col_iota = sb("col_iota", [P, WMAX])
        rows = sb("rows", [P, ROWS, F])
        hi = sb("hi", [P, RING, F], F32R)
        lo = sb("lo", [P, RING, F], F32R)
        onehot = sb("onehot", [P, RING, WMAX], F32R)
        xr = sb("xr", [P, F])
        z = sb("z", [P, F])
        z_stat = sb("z_stat", [P, 6])
        z_mv = sb("z_mv", [P, 2])
        z_std = sb("z_std", [P, 1])
        z_rstd = sb("z_rstd", [P, 1])
        z_out = sb("z_out", [P, F])
        flag_f = sb("flag_f", [1, 1])
        flag_i = sb("flag_i", [1, 1], I32)
        w_raw = sb("w_raw", [P, 2, KH, F])
        w_hi = sbf("w_hi", [P, R, KH, F], F32R)
        w_lo = sbf("w_lo", [P, R, KH, F], F32R)
        a_hi = sbf("a_hi", [P, 2, KH, R, SB], F32R)
        a_lo = sbf("a_lo", [P, 2, KH, R, SB], F32R)
        fast.close()
        w_sb = sb("w_sb", [P, R, KH, F])
        g_src = sb("g_src", [P, 1], I32)
        g_dst = sb("g_dst", [P, 1], I32)
        g_rel = sb("g_rel", [P, 1], I32)
        g_norm = sb("g_norm", [P, 1])
        g_dstf = sb("g_dstf", [P, 1])
        g_relf = sb("g_relf", [P, 1])
        g_dstw = sb("g_dstw", [P, P])
        g_rows = sb("g_rows", [P, F])
        g_cur = sb("g_cur", [P, F])
        g_msg = sb("g_msg", [P, F])
        g_msgT = sb("g_msgT", [P, KH, P])
        g_mask = sb("g_mask", [P, R])
        g_y = sb("g_y", [P, F])
        g_eq = sb("g_eq", [P, P])
        g_dup = sb("g_dup", [P, P])
        g_ndup = sb("g_ndup", [P, 1])
        g_to = sb("g_to", [P, 1])
        g_toi = sb("g_toi", [P, 1], I32)
        n_stat = sb("n_stat", [P, 6])
        n_mv = sb("n_mv", [P, 2])
        n_std = sb("n_std", [P, 1])
        n_rstd = sb("n_rstd", [P, 1])
        n_out = sb("n_out", [P, F])

        ps_a = ctx.enter_context(nc.psum_tensor("ps_a", [P, OPEN, KH, GN * R], F32))
        ps_m = ctx.enter_context(nc.psum_tensor("ps_m", [P, 512], F32))
        ps_f = ctx.enter_context(nc.psum_tensor("ps_f", [P, 512], F32))
        ps_z = ctx.enter_context(nc.psum_tensor("ps_z", [P, 2, 512], F32))
        ps_t = ps_m[:, 0:KH * P].rearrange("p (k e) -> p k e", k=KH)
        ps_d = ps_z[:, 1, 0:P]
        ps_r = ps_a[:, :, 0, :]
        ps_s = ps_z[:, 0, 0:F]

        general_weights_in = sem("general_weights_in")
        constants_made = sem("constants_made")
        acc_filled = sem("acc_filled")
        general_started = sem("general_started")
        tile_edges_in = sem("tile_edges_in")
        src_rows_in = sem("src_rows_in")
        dst_rows_in = sem("dst_rows_in")
        messages_turned = sem("messages_turned")
        messages_copied = sem("messages_copied")
        relation_multiplied = sem("relation_multiplied")
        relation_added = sem("relation_added")
        sums_made = sem("sums_made")
        rows_updated = sem("rows_updated")
        rows_stored = sem("rows_stored")
        general_steps = sem("general_steps")
        norm_rows_in = sem("norm_rows_in")
        norm_deviation_made = sem("norm_deviation_made")
        norm_variance_made = sem("norm_variance_made")
        norm_rows_made = sem("norm_rows_made")
        norm_rows_stored = sem("norm_rows_stored")
        tile_ended = sem("tile_ended")
        ticks = sem("ticks")

        samples_in = sem("samples_in")
        tail_written = sem("tail_written")
        padding_made = sem("padding_made")
        samples_compared = sem("samples_compared")
        samples_counted = sem("samples_counted")
        hit_row_made = sem("hit_row_made")
        hit_row_in = sem("hit_row_in")
        first_edge_made = sem("first_edge_made")
        first_edge_turned = sem("first_edge_turned")
        first_edges_ready = sem("first_edges_ready")
        edges_in = sem("edges_in")
        edges_converted = sem("edges_converted")
        edges_turned = sem("edges_turned")
        edges_copied = sem("edges_copied")
        keys_made = sem("keys_made")
        upper_made = sem("upper_made")
        tile_parts_made = sem("tile_parts_made")
        tiles_summed = sem("tiles_summed")
        a_upper_made = sem("a_upper_made")
        products_made = sem("products_made")
        own_rows_in = sem("own_rows_in")
        residual_added = sem("residual_added")
        variance_steps = sem("variance_steps")
        deviation_made = sem("deviation_made")
        rows_normalised = sem("rows_normalised")
        rows_out = sem("rows_out")
        seek_steps = sem("seek_steps")
        flag_steps = sem("flag_steps")
        blocks_counted = sem("blocks_counted")
        count_ended = sem("count_ended")
        rstd_made = sem("rstd_made")
        key_steps = sem("key_steps")
        window_bases_made = sem("window_bases_made")
        window_widths_made = sem("window_widths_made")
        columns_made = sem("columns_made")
        optional_rows_in = sem("optional_rows_in")
        optional_hits_ready = sem("optional_hits_ready")
        optional_hits_summed = sem("optional_hits_summed")
        w_upper_made = sem("w_upper_made")
        w_lower_made = sem("w_lower_made")
        a_lower_made = sem("a_lower_made")
        rows_in = [sem(f"rows_in{t}") for t in range(CT)]
        weights_in = [sem(f"weights_in{n}") for n in range(2)]

        block = ctx.enter_context(nc.Block())
        G = slice(0, ET)

        def at(b, per, more):
            u, k = b
            return k * per + more if u is None else u * (2 * per) + (k * per + more)

        def wait(eng, s, b, per, more):
            if b[0] is None and at(b, per, more) <= 0:
                return
            eng.wait_ge(s, at(b, per, more))

        def blocks(eng, one):
            one((None, 0), True, False, False)
            one((None, 1), True, True, False)
            one((None, 2), True, True, True)
            with eng.Fori(1, (NB - 1) // 2) as u:
                one((u, 1), True, True, True)
                one((u, 2), True, True, True)
            one((None, NB), False, True, True)
            one((None, NB + 1), False, False, True)

        def rows_slot(b, t):
            return (b[1] * CT + t) % ROWS

        def ring_slot(b, t):
            return (b[1] * CT + t) % RING


        def fast_sync(sp):
            def load_edges(first, arrays):
                for a, v in enumerate(arrays):
                    sp.dma_start(raw[:, a, :], v[bass.ds(first, CE)].rearrange("(j p) -> j p", p=P)).then_inc(
                        edges_in, 16)

            def raw_left(b):
                sp.wait_ge(edges_converted, b)
                sp.wait_ge(edges_turned, b)

            def load_weights(n):
                if n >= 2:
                    sp.wait_ge(w_lower_made, n - 1)
                sp.dma_start(w_raw[:, n % 2, :, :], weight[n, :, :].rearrange("(k p) n -> p k n", p=P)).then_inc(
                    weights_in[n % 2], 16)

            edges = (src, dst, rel, norm_i)
            tails = [tail[a, :] for a in range(4)]
            load_edges(0, edges)
            sp.dma_start(sample_i[0:SP, :], dst.rearrange("(p c e) -> p c e", c=SC, e=SROW)[:, :, 0],
                         allow_slow_non_contiguous=True).then_inc(samples_in, 16)
            sp.dma_start(xr[:, :], x[0:SB, :]).then_inc(own_rows_in, 16)
            for n in range(WEIGHTS_BEFORE):
                load_weights(n)
            sp.wait_ge(first_edges_ready, 1)
            raw_left(1)
            load_edges(sp.value_load(first_i[0:1, 1:2], min_val=0, max_val=E - CE), edges)
            for n in range(WEIGHTS_BEFORE, R):
                load_weights(n)
            raw_left(2)
            load_edges(sp.value_load(first_i[0:1, 2:3], min_val=0, max_val=E - CE), edges)
            for a, v in enumerate(edges):
                sp.dma_start(tail[a, 0:TAIL].rearrange("(p e) -> p e", p=64),
                             v[E - TAIL:E].rearrange("(p e) -> p e", p=64)).then_inc(tail_written, 16)
            sp.wait_ge(padding_made, 2)
            for a in range(4):
                sp.dma_start(tail[a, TAIL:TAIL + CE].rearrange("(p e) -> p e", p=64),
                             pad_i[:, int(a == 1), :]).then_inc(tail_written, 16)
            with sp.Fori(1, NB - 3) as b:
                raw_left(b + 2)
                sp.sem_inc(ticks, 1)
                load_edges(sp.value_load(first_i[0:1, bass.ds(b + 2, 1)], min_val=0, max_val=E - CE), edges)
                sp.wait_ge(rows_normalised, b)
                sp.sem_inc(ticks, 1)
                sp.dma_start(out[bass.ds(b * SB - SB, SB), :], z_out[:, :]).then_inc(rows_out, 16)
                sp.dma_start(xr[:, :], x[bass.ds(b * SB, SB), :]).then_inc(own_rows_in, 16)
            for b in range(NB - 3, NB):
                if b == NB - 3:
                    sp.wait_ge(tail_written, 8 * 16)
                    raw_left(NB - 1)
                    load_edges(sp.value_load(first_i[0:1, NB - 1:NB], min_val=0, max_val=TAIL), tails)
                if b == NB - 2:
                    raw_left(NB)
                    load_edges(TAIL, tails)
                sp.wait_ge(rows_normalised, b)
                rows_of = min(SB, N - b * SB)
                sp.dma_start(out[(b - 1) * SB:b * SB, :], z_out[:, :]).then_inc(rows_out, 16)
                sp.dma_start(xr[0:rows_of, :], x[b * SB:b * SB + rows_of, :]).then_inc(own_rows_in, 16)
            sp.wait_ge(rows_normalised, NB)
            sp.dma_start(out[(NB - 1) * SB:N, :], z_out[0:LAST, :]).then_inc(rows_out, 16)
            sp.wait_ge(rows_out, NB * 16)

        def fast_pool(pool):
            pool.memset(ident[:, :], 0.0).then_inc(constants_made, 1)
            pool.iota(bound_row[:, :], [[SB, NB]], base=0, channel_multiplier=0,
                      allow_small_or_imprecise_dtypes=True).then_inc(constants_made, 1)
            pool.iota(bound_col[:, :], [[0, 1]], base=0, channel_multiplier=SB,
                      allow_small_or_imprecise_dtypes=True).then_inc(constants_made, 1)
            pool.wait_ge(constants_made, 3)
            pool.affine_select(out=ident[:, :], in_=ident[:, :], compare_op=ALU.not_equal, fill=1.0,
                               base=0, pattern=[[-1, P]], channel_multiplier=1).then_inc(constants_made, 1)
            pool.memset(pad_i[:, 0, :], 0).then_inc(padding_made, 1)
            pool.memset(pad_i[:, 1, :], PAD_DST).then_inc(padding_made, 1)
            pool.iota(block_base[:, :], [[SB * R, NB + 1]], base=0, channel_multiplier=0,
                      allow_small_or_imprecise_dtypes=True).then_inc(constants_made, 1)
            pool.iota(col_iota[:, :], [[1, WMAX]], base=0, channel_multiplier=0,
                      allow_small_or_imprecise_dtypes=True).then_inc(constants_made, 1)
            for width, t0, t1 in runs([(end - first) * R for first, end in WIN]):
                pool.memset(win_width[:, t0:t1], float(width)).then_inc(window_widths_made, 1)
            gathered = [pool.alloc_register(f"gathered{t}") for t in OPTIONAL]
            last_row = pool.to_reg(N - 1)

            def gather(b, t):
                pool.indirect_dma_start(rows[:, rows_slot(b, t), :], None, x,
                                        bass.IndirectOffsetOnAxis(ap=idx[:, b[1] % 2, t:t + 1], axis=0),
                                        bounds_check=last_row, oob_is_err=False).then_inc(rows_in[t], 16)

            def confirm():
                for t, arrived in zip(OPTIONAL, gathered):
                    pool.wait_ge(rows_in[t], arrived)
                pool.sem_inc(optional_rows_in, 1)

            def gather_block(b, sums, products, rows_):
                if not sums:
                    return
                for t in range(CT):
                    if t == 0:
                        wait(pool, keys_made, b, 1, 1)
                    if t % BATCH == 0:
                        wait(pool, tile_parts_made, b, 2 * CT, 2 * (t + BATCH - ROWS))
                        pool.sem_inc(ticks, 1)
                    if t == CONFIRM and not (b[0] is None and b[1] == 0):
                        confirm()
                    if b[0] is None and b[1] == 0:
                        if t == SEEK_GATHER:
                            pool.wait_ge(hit_row_made, 1)
                            pool.indirect_dma_start(hit_dst[0:NB, :], None, dst.rearrange("(r e) -> r e", e=SROW),
                                                    bass.IndirectOffsetOnAxis(ap=hit_row_i[0:NB, :], axis=0),
                                                    bounds_check=SROWS - 1, oob_is_err=False).then_inc(hit_row_in, 16)
                        gather(b, t)
                        if t in OPTIONAL:
                            pool.reg_mov(gathered[OPTIONAL.index(t)], 16)
                    elif t in OPTIONAL:
                        n = OPTIONAL.index(t)
                        if n == 0:
                            wait(pool, optional_hits_ready, b, 1, 0)
                            pool.sem_inc(ticks, 1)
                        edges = pool.value_load(late_hits[0:1, b[1] % 2, n:n + 1], min_val=0, max_val=P)
                        with pool.If(edges > 0):
                            gather(b, t)
                            pool.reg_add(gathered[n], gathered[n], 16)
                    else:
                        gather(b, t)

            blocks(pool, gather_block)
            confirm()

        def fast_vector(dve):
            seek_step = count(1)

            def done(ins):
                ins.then_inc(seek_steps, 1)
                dve.wait_ge(seek_steps, next(seek_step))

            def seek_samples():
                dve.wait_ge(samples_in, 16)
                done(dve.tensor_copy(sample[0:SP, :], sample_i[0:SP, :]))
                for c in range(SC):
                    dve.tensor_scalar(below[0:SP, c, :], bound_row[0:SP, :], sample[0:SP, c:c + 1], None,
                                      ALU.is_gt).then_inc(samples_compared, 1)

            B = slice(0, NB)

            def seek_row():
                dve.wait_ge(samples_counted, 1)
                done(dve.tensor_scalar(hit_row[B, :], ps_f[B, 0:1], -1.0, 0.0, ALU.add, ALU.max))
                dve.tensor_copy(hit_row_i[B, :], hit_row[B, :]).then_inc(hit_row_made, 1)

            def seek_edge():
                dve.wait_ge(hit_row_in, 16)
                done(dve.tensor_scalar(hit_cmp[B, :], hit_dst[B, :], bound_col[B, :], None, ALU.is_lt))
                done(dve.reduce_sum(hit_cnt[B, :], hit_cmp[B, :], axis=AX_X))
                dve.scalar_tensor_tensor(out=first_edge[B, :], in0=hit_row[B, :], scalar=float(SROW),
                                         in1=hit_cnt[B, :], op0=ALU.mult, op1=ALU.add).then_inc(first_edge_made, 1)

            def seek_table():
                dve.wait_ge(first_edge_turned, 1)
                done(dve.tensor_scalar(first_row[0:1, 0:NB - 1], ps_f[0:1, FIRST_AT:FIRST_AT + NB - 1], float(E - CE),
                                       None, ALU.min))
                done(dve.tensor_scalar(first_row[0:1, NB - 1:NB], ps_f[0:1, FIRST_AT + NB - 1:FIRST_AT + NB],
                                       float(-(E - TAIL)), 0.0, ALU.add, ALU.max))
                dve.tensor_copy(first_i[0:1, :], first_row[0:1, :]).then_inc(first_edges_ready, 1)

            def split_edges(b):
                wait(dve, edges_in, b, 64, 64)
                wait(dve, edges_turned, b, 1, 0)
                dve.tensor_copy(raw_f[:, :, :], raw[:, 0:3, :]).then_inc(edges_converted, 1)

            def keys(b):
                k = b[1] % 2
                wait(dve, edges_copied, b, 1, 1)
                m = meta[:, k, :, :]
                dve.tensor_copy(idx[:, k, :], m[:, 0, :]).then_inc(key_steps, 1)
                dve.scalar_tensor_tensor(out=key_a[:, :], in0=m[:, 1, :], scalar=float(R), in1=m[:, 2, :],
                                         op0=ALU.mult, op1=ALU.add).then_inc(key_steps, 1)
                wait(dve, key_steps, b, 6, 2)
                base = block_base[:, b[1]:b[1] + 1] if b[0] is None else block_base[:, bass.ds(b[0] * 2 + b[1], 1)]
                dve.scalar_tensor_tensor(out=key[:, k, :], in0=key_a[:, :], scalar=base, in1=win_base[:, :],
                                         op0=ALU.subtract, op1=ALU.subtract).then_inc(key_steps, 1)
                wait(dve, key_steps, b, 6, 3)
                dve.sem_inc(keys_made, 1)
                dve.tensor_tensor(key_in[:, :], key[:, k, :], win_width[:, :], ALU.is_lt).then_inc(key_steps, 1)
                wait(dve, key_steps, b, 6, 4)
                wait(dve, optional_hits_summed, b, 1, -1)
                dve.scalar_tensor_tensor(out=key_hit[:, :], in0=key[:, k, :], scalar=0.0, in1=key_in[:, :],
                                         op0=ALU.is_ge, op1=ALU.mult).then_inc(key_steps, 1)
                wait(dve, key_steps, b, 6, 5)
                dve.reduce_sum(hits[:, :], key_hit[:, :], axis=AX_X).then_inc(key_steps, 1)
                wait(dve, key_steps, b, 6, 6)
                dve.tensor_tensor(total[:, :], total[:, :], hits[:, :], ALU.add).then_inc(blocks_counted, 1)

            def convert_hits(b):
                wait(dve, optional_hits_summed, b, 1, 0)
                dve.tensor_copy(late_hits[0:1, b[1] % 2, :], ps_f[0:1, HITS_AT:HITS_AT + len(OPTIONAL)]).then_inc(
                    optional_hits_ready, 1)

            def normalise(b):
                wait(dve, products_made, b, 1, -1)
                wait(dve, own_rows_in, b, 16, -16)
                dve.tensor_tensor(z[:, :], xr[:, :], ps_z[:, b[1] % 2, 0:F], ALU.add).then_inc(residual_added, 1)
                wait(dve, residual_added, b, 1, -1)
                dve.bn_stats(z_stat[:, :], z[:, :]).then_inc(variance_steps, 1)
                wait(dve, variance_steps, b, 2, -3)
                dve.sem_inc(ticks, 1)
                dve.bn_aggr(z_mv[:, :], z_stat[:, :]).then_inc(variance_steps, 1)
                wait(dve, deviation_made, b, 1, -1)
                dve.reciprocal(z_rstd[:, :], z_std[:, :]).then_inc(rstd_made, 1)
                wait(dve, rstd_made, b, 1, -1)
                wait(dve, rows_out, b, 16, -32)
                dve.tensor_scalar(z_out[:, :], z[:, :], z_mv[:, 0:1], z_rstd[:, :],
                                  ALU.subtract, ALU.mult).then_inc(rows_normalised, 1)

            def lower_part(b, g):
                for h in range(KH):
                    wait(dve, a_upper_made, b, GROUPS * KH, KH * g + h + 1)
                    at_g = slice(g * GN, (g + 1) * GN)
                    dve.tensor_tensor(a_lo[:, b[1] % 2, h, :, at_g],
                                      ps_a[:, g % OPEN, h, :].rearrange("p (n r) -> p r n", r=R),
                                      a_hi[:, b[1] % 2, h, :, at_g].bitcast(F32), ALU.subtract).then_inc(
                                          a_lower_made, 1)

            def tile_block(b, sums, products, rows_):
                for t in range(CT):
                    if sums:
                        slot = ring_slot(b, t)
                        if not products and t in WEIGHTS_AT:
                            n = WEIGHTS_AT[t]
                            dve.wait_ge(w_upper_made, n + 1)
                            dve.tensor_tensor(w_lo[:, n, :, :], w_raw[:, n % 2, :, :],
                                              w_hi[:, n, :, :].bitcast(F32), ALU.subtract).then_inc(w_lower_made, 1)
                        if t == prepare(b)[0]:
                            next_edges(split_edges, b)
                        if t == prepare(b)[3]:
                            next_edges(keys, b)
                        if t == prepare(b)[5]:
                            next_edges(convert_hits, b)
                        if not products and t in seek:
                            seek[t]()
                        first, end = WIN[t]
                        wait(dve, tiles_summed, b, CT, t + 1 - RING)
                        dve.tensor_scalar(onehot[:, slot, 0:(end - first) * R], col_iota[:, 0:(end - first) * R],
                                          key[:, b[1] % 2, t:t + 1], None, ALU.is_equal).then_inc(tile_parts_made, 1)
                        wait(dve, upper_made, b, CT, t + 1)
                        dve.scalar_tensor_tensor(out=lo[:, slot, :], in0=rows[:, rows_slot(b, t), :],
                                                 scalar=meta[:, b[1] % 2, 3, t:t + 1],
                                                 in1=hi[:, slot, :].bitcast(F32), op0=ALU.mult,
                                                 op1=ALU.subtract).then_inc(tile_parts_made, 1)
                    for g in range(GROUPS):
                        due = group_tiles[g][1] + EVAC_LAG + 1
                        if sums and t == due:
                            lower_part(b, g)
                        if products and t == due - CT:
                            lower_part((b[0], b[1] - 1), g)
                    if rows_ and t == NORM_AT:
                        normalise(b)

            for base, t0, t1 in runs([first * R for first, _ in WIN]):
                dve.memset(win_base[:, t0:t1], float(base)).then_inc(window_bases_made, 1)
            dve.memset(total[:, :], 0.0).then_inc(window_bases_made, 1)
            dve.memset(ones[:, :], 1.0).then_inc(columns_made, 1)
            dve.memset(eps_col[:, :], EPS).then_inc(columns_made, 1)
            split_edges((None, 0))
            dve.wait_ge(window_bases_made, len(runs([first for first, _ in WIN])) + 1)
            dve.wait_ge(window_widths_made, len(runs([end - first for first, end in WIN])))
            dve.wait_ge(constants_made, 6)
            keys((None, 0))
            seek_samples()
            seek = {SEEK_ROW: seek_row, SEEK_EDGE: seek_edge, SEEK_TABLE: seek_table}
            blocks(dve, tile_block)
            dve.wait_ge(blocks_counted, NB + 1)
            dve.sem_inc(count_ended, 1)
            dve.wait_ge(flag_steps, 1)
            dve.tensor_scalar(flag_f[:, :], ps_f[0:1, TOTAL_AT:TOTAL_AT + 1], float(E), None,
                              ALU.not_equal).then_inc(flag_steps, 1)
            dve.wait_ge(flag_steps, 2)
            dve.tensor_copy(flag_i[:, :], flag_f[:, :]).then_inc(flag_steps, 1)

        def runs(values):
            starts = [n for n, v in enumerate(values) if n == 0 or v != values[n - 1]]
            return [(values[n], n, m) for n, m in zip(starts, starts[1:] + [len(values)])]

        def prepare(b):
            return PREPARE_0 if b[0] is None and b[1] == 0 else PREPARE

        def next_edges(step, b):
            step((b[0], b[1] + 1))

        def fast_scalar(act):
            def copy_edges(b):
                k = b[1] % 2
                wait(act, edges_turned, b, 1, 1)
                wait(act, tile_parts_made, b, 2 * CT, -2 * CT)
                act.activation(meta[:, k, :, :], ps_m[:, 0:4 * CT].rearrange("p (a t) -> p a t", a=4),
                               ACT.Copy).then_inc(edges_copied, 1)

            def evacuate(b, g):
                wait(act, tiles_summed, b, CT, group_tiles[g][1] + 1)
                if g == 0:
                    wait(act, products_made, b, 1, -1)
                for h in range(KH):
                    act.activation(a_hi[:, b[1] % 2, h, :, g * GN:(g + 1) * GN],
                                   ps_a[:, g % OPEN, h, :].rearrange("p (n r) -> p r n", r=R),
                                   ACT.Copy).then_inc(a_upper_made, 1)

            def tile_block(b, sums, products, rows_):
                for t in range(CT):
                    if sums:
                        if not products and t in WEIGHTS_AT:
                            n = WEIGHTS_AT[t]
                            act.wait_ge(weights_in[n % 2], 16 * (n // 2 + 1))
                            act.activation(w_hi[:, n, :, :], w_raw[:, n % 2, :, :], ACT.Copy).then_inc(
                                w_upper_made, 1)
                        if t == prepare(b)[2]:
                            next_edges(copy_edges, b)
                        slot = ring_slot(b, t)
                        if t in OPTIONAL:
                            wait(act, optional_rows_in, b, 1, 1)
                        else:
                            wait(act, rows_in[t], b, 16, 16)
                        wait(act, tiles_summed, b, CT, t + 1 - RING)
                        if t == 0:
                            wait(act, edges_copied, b, 1, 1)
                        act.activation(hi[:, slot, :], rows[:, rows_slot(b, t), :], ACT.Copy,
                                       scale=meta[:, b[1] % 2, 3, t:t + 1]).then_inc(upper_made, 1)
                    for g in range(GROUPS):
                        due = group_tiles[g][1] + EVAC_LAG
                        if sums and t == due:
                            evacuate(b, g)
                        if products and t == due - CT:
                            evacuate((b[0], b[1] - 1), g)
                    if rows_ and t == NORM_AT:
                        if b[0] is None and b[1] == 2:
                            act.wait_ge(columns_made, 2)
                        wait(act, variance_steps, b, 2, -2)
                        act.activation(z_std[:, :], z_mv[:, 1:2], ACT.Sqrt, bias=eps_col[:, :]).then_inc(
                            deviation_made, 1)

            copy_edges((None, 0))
            blocks(act, tile_block)

        def fast_tensor(pe):
            def seek_count():
                pe.wait_ge(columns_made, 2)
                pe.wait_ge(samples_compared, SC)
                for c in range(SC):
                    ins = pe.matmul(ps_f[0:NB, 0:1], below[0:SP, c, :], ones[0:SP, :], start=c == 0,
                                    stop=c == SC - 1)
                ins.then_inc(samples_counted, 1)

            def seek_turn():
                pe.wait_ge(first_edge_made, 1)
                pe.transpose(ps_f[0:1, FIRST_AT:FIRST_AT + NB], first_edge[0:NB, :], ident[0:NB, 0:NB]).then_inc(
                    first_edge_turned, 1)

            def sum_hits(b):
                wait(pe, key_steps, b, 6, 5)
                wait(pe, optional_hits_ready, b, 1, -1)
                pe.matmul(ps_f[0:1, HITS_AT:HITS_AT + len(OPTIONAL)], ones[:, :],
                          key_hit[:, OPTIONAL[0]:OPTIONAL[-1] + 1], start=True, stop=True).then_inc(optional_hits_summed, 1)

            def turn_edges(b):
                wait(pe, edges_converted, b, 1, 1)
                wait(pe, edges_copied, b, 1, 0)
                pe.sem_inc(ticks, 1)
                for a in range(4):
                    v = raw_f[:, a, :] if a < 3 else raw[:, a, :].bitcast(F32)
                    ins = pe.transpose(ps_m[:, a * CT:(a + 1) * CT], v, ident[0:CT, 0:CT])
                ins.then_inc(edges_turned, 1)

            def product(b, n):
                r, h = n // KH, n % KH
                if n == 0:
                    if b[0] is None and b[1] == 1:
                        pe.wait_ge(w_lower_made, R)
                    wait(pe, a_lower_made, b, GROUPS * KH, 0)
                    wait(pe, residual_added, b, 1, -2)
                terms = ((a_hi, w_hi), (a_hi, w_lo), (a_lo, w_hi))
                for m, (a_part, w_part) in enumerate(terms):
                    ins = pe.matmul(ps_z[:, (b[1] + 1) % 2, 0:F], a_part[:, (b[1] + 1) % 2, h, r, :],
                                    w_part[:, r, h, :], start=n == 0 and m == 0,
                                    stop=n == KH * R - 1 and m == len(terms) - 1)
                if n == KH * R - 1:
                    ins.then_inc(products_made, 1)

            def tile_block(b, sums, products, rows_):
                n = 0
                for t in range(CT):
                    if sums:
                        slot = ring_slot(b, t)
                        if t == prepare(b)[1]:
                            next_edges(turn_edges, b)
                        if t == prepare(b)[4]:
                            next_edges(sum_hits, b)
                        if t == SEEK_TURN and not products:
                            seek_turn()
                        wait(pe, tile_parts_made, b, 2 * CT, 2 * t + 2)
                        first, end = WIN[t]
                        groups = [g for g in range(GROUPS) if first < (g + 1) * GN and end > g * GN]
                        for h in range(KH):
                            for g in groups:
                                if group_tiles[g][0] == t:
                                    wait(pe, a_lower_made, b, GROUPS * KH, KH * (g - OPEN) + h + 1)
                            for part in (hi, lo):
                                for g in groups:
                                    begin, stop = max(first, g * GN), min(end, (g + 1) * GN)
                                    opens = group_tiles[g][0] == t and part is hi
                                    ins = pe.matmul(
                                        ps_a[:, g % OPEN, h, (begin - g * GN) * R:(stop - g * GN) * R],
                                        part[:, slot, h * P:(h + 1) * P],
                                        onehot[:, slot, (begin - first) * R:(stop - first) * R],
                                        start=opens, stop=False, skip_group_check=True)
                        ins.then_inc(tiles_summed, 1)
                    if products:
                        for _ in range(products_after[t]):
                            product(b, n)
                            n += 1

            pe.wait_ge(constants_made, 4)
            turn_edges((None, 0))
            seek_count()
            blocks(pe, tile_block)
            pe.wait_ge(count_ended, 1)
            pe.matmul(ps_f[0:1, TOTAL_AT:TOTAL_AT + 1], total[:, :], ones[:, :], start=True, stop=True).then_inc(
                flag_steps, 1)

        def uncounted(eng):
            eng.wait_ge(flag_steps, 3)
            return eng.value_load(flag_i[0:1, 0:1], min_val=0, max_val=1)


        def general_sync(sp):
            sp.dma_start(acc, x).then_inc(acc_filled, 16)
            sp.dma_start(w_sb[:, :, :, :], weight.rearrange("r (k p) n -> p r k n", p=P)).then_inc(
                general_weights_in, 16)
            sp.wait_ge(general_started, 1)
            sp.wait_ge(acc_filled, 16)
            with sp.Fori(0, NT) as i:
                sp.wait_ge(tile_ended, i + 1)
                sp.sem_inc(ticks, 1)
                at = bass.ds(i * ET, ET)
                sp.dma_start(g_src[G, :], src[at].rearrange("(p a) -> p a", a=1)).then_inc(tile_edges_in, 16)
                sp.dma_start(g_dst[G, :], dst[at].rearrange("(p a) -> p a", a=1)).then_inc(tile_edges_in, 16)
                sp.dma_start(g_rel[G, :], rel[at].rearrange("(p a) -> p a", a=1)).then_inc(tile_edges_in, 16)
                sp.dma_start(g_norm[G, :], norm[at, :]).then_inc(tile_edges_in, 16)
            sp.wait_ge(tile_ended, NT + 1)
            with sp.Fori(0, NN) as t:
                sp.dma_start(g_rows[0:NR, :], acc[bass.ds(t * NR, NR), :]).then_inc(norm_rows_in, 16)
                sp.wait_ge(norm_rows_made, t + 1)
                sp.sem_inc(ticks, 1)
                sp.dma_start(out[bass.ds(t * NR, NR), :], n_out[0:NR, :]).then_inc(norm_rows_stored, 16)
                sp.wait_ge(norm_rows_stored, t * 16 + 16)
                sp.sem_inc(ticks, 1)

        def general_pool(pool):
            pool.memset(earlier[:, :], 1.0).then_inc(constants_made, 1)
            pool.iota(rel_iota[:, :], [[1, R]], base=0, channel_multiplier=0,
                      allow_small_or_imprecise_dtypes=True).then_inc(constants_made, 1)
            pool.wait_ge(constants_made, 8)
            pool.affine_select(out=earlier[:, :], in_=earlier[:, :], compare_op=ALU.is_gt, fill=0.0,
                               base=0, pattern=[[-1, P]], channel_multiplier=1).then_inc(constants_made, 1)
            pool.sem_inc(tile_ended, 1)
            pool.sem_inc(general_started, 1)
            pool.wait_ge(acc_filled, 16)
            last_row = pool.to_reg(N - 1)
            with pool.Fori(0, NT) as i:
                pool.wait_ge(tile_edges_in, i * 64 + 64)
                pool.sem_inc(ticks, 1)
                pool.indirect_dma_start(g_rows[G, :], None, x, bass.IndirectOffsetOnAxis(ap=g_src[G, :], axis=0),
                                        bounds_check=last_row, oob_is_err=False).then_inc(src_rows_in, 16)
                pool.indirect_dma_start(g_cur[G, :], None, acc, bass.IndirectOffsetOnAxis(ap=g_dst[G, :], axis=0),
                                        bounds_check=last_row, oob_is_err=False).then_inc(dst_rows_in, 16)
                pool.wait_ge(rows_updated, i + 1)
                pool.sem_inc(ticks, 1)
                pool.indirect_dma_start(acc, bass.IndirectOffsetOnAxis(ap=g_toi[G, :], axis=0), g_cur[G, :], None,
                                        bounds_check=last_row, oob_is_err=False).then_inc(rows_stored, 16)
                pool.wait_ge(rows_stored, i * 16 + 16)
                pool.sem_inc(tile_ended, 1)

        def general_vector(dve):
            dve.wait_ge(constants_made, 9)
            with dve.Fori(0, NT) as i:
                c = i * 11

                def done(ins):
                    ins.then_inc(general_steps, 1)

                dve.wait_ge(tile_edges_in, i * 64 + 64)
                done(dve.tensor_copy(g_dstf[G, :], g_dst[G, :]))
                done(dve.tensor_copy(g_relf[G, :], g_rel[G, :]))
                dve.wait_ge(general_steps, c + 2)
                done(dve.tensor_scalar(g_mask[G, :], rel_iota[G, :], g_relf[G, :], None, ALU.is_equal))
                done(dve.tensor_scalar(g_dstw[G, 0:ET], ident[G, 0:ET], 0.0, g_dstf[G, :], ALU.mult, ALU.add))
                dve.wait_ge(src_rows_in, i * 16 + 16)
                done(dve.tensor_scalar(g_msg[G, :], g_rows[G, :], g_norm[G, :], None, ALU.mult))
                dve.wait_ge(messages_turned, i * 3 + 3)
                done(dve.tensor_scalar(g_eq[G, 0:ET], ps_d[G, 0:ET], g_dstf[G, :], None, ALU.is_equal))
                dve.wait_ge(general_steps, c + 6)
                done(dve.tensor_tensor(g_dup[G, 0:ET], g_eq[G, 0:ET], earlier[G, 0:ET], ALU.mult))
                dve.wait_ge(general_steps, c + 7)
                done(dve.reduce_sum(g_ndup[G, :], g_dup[G, 0:ET], axis=mybir.AxisListType.X))
                dve.wait_ge(general_steps, c + 8)
                done(dve.scalar_tensor_tensor(out=g_to[G, :], in0=g_ndup[G, :], scalar=float(2 ** 16),
                                              in1=g_dstf[G, :], op0=ALU.mult, op1=ALU.add))
                dve.wait_ge(general_steps, c + 9)
                done(dve.tensor_copy(g_toi[G, :], g_to[G, :]))
                for r in range(R):
                    dve.wait_ge(relation_multiplied, i * R + r + 1)
                    if r == 0:
                        dve.tensor_scalar(g_y[G, :], ps_r[G, r % 2, 0:F], g_mask[G, r:r + 1], None,
                                          ALU.mult).then_inc(relation_added, 1)
                    else:
                        dve.wait_ge(relation_added, i * R + r)
                        dve.scalar_tensor_tensor(out=g_y[G, :], in0=ps_r[G, r % 2, 0:F], scalar=g_mask[G, r:r + 1],
                                                 in1=g_y[G, :], op0=ALU.mult, op1=ALU.add).then_inc(relation_added, 1)
                dve.wait_ge(sums_made, i + 1)
                dve.wait_ge(dst_rows_in, i * 16 + 16)
                done(dve.tensor_tensor(g_cur[G, :], g_cur[G, :], ps_s[G, :], ALU.add))
                dve.wait_ge(general_steps, c + 11)
                dve.sem_inc(rows_updated, 1)
            L = slice(0, NR)
            with dve.Fori(0, NN) as t:
                dve.wait_ge(norm_rows_in, t * 16 + 16)
                c = NT * 11 + t * 4
                dve.bn_stats(n_stat[L, :], g_rows[L, :]).then_inc(general_steps, 1)
                dve.wait_ge(general_steps, c + 1)
                dve.sem_inc(ticks, 1)
                dve.bn_aggr(n_mv[L, :], n_stat[L, :]).then_inc(general_steps, 1)
                dve.wait_ge(general_steps, c + 2)
                dve.sem_inc(norm_variance_made, 1)
                dve.wait_ge(norm_deviation_made, t + 1)
                dve.reciprocal(n_rstd[L, :], n_std[L, :]).then_inc(general_steps, 1)
                dve.wait_ge(general_steps, c + 3)
                dve.tensor_scalar(n_out[L, :], g_rows[L, :], n_mv[L, 0:1], n_rstd[L, :],
                                  ALU.subtract, ALU.mult).then_inc(general_steps, 1)
                dve.wait_ge(general_steps, c + 4)
                dve.sem_inc(norm_rows_made, 1)

        def general_scalar(act):
            with act.Fori(0, NT) as i:
                act.wait_ge(messages_turned, i * 3 + 2)
                act.activation(g_msgT[:, :, 0:ET], ps_t[:, :, 0:ET], ACT.Copy).then_inc(messages_copied, 1)
            with act.Fori(0, NN) as t:
                act.wait_ge(norm_variance_made, t + 1)
                act.activation(n_std[0:NR, :], n_mv[0:NR, 1:2], ACT.Sqrt, bias=eps_col[0:NR, :]).then_inc(
                    norm_deviation_made, 1)

        def general_tensor(pe):
            pe.wait_ge(general_weights_in, 16)
            with pe.Fori(0, NT) as i:
                pe.wait_ge(general_steps, i * 11 + 5)
                for k in range(KH):
                    pe.transpose(ps_t[:, k, 0:ET], g_msg[G, k * P:(k + 1) * P], ident[G, 0:ET]).then_inc(
                        messages_turned, 1)
                pe.transpose(ps_d[G, 0:ET], g_dstw[G, 0:ET], ident[G, 0:ET]).then_inc(messages_turned, 1)
                pe.wait_ge(messages_copied, i + 1)
                for r in range(R):
                    if r >= 2:
                        pe.wait_ge(relation_added, i * R + r - 1)
                    for k in range(KH):
                        ins = pe.matmul(ps_r[G, r % 2, 0:F], g_msgT[:, k, 0:ET], w_sb[:, r, k, :],
                                        start=k == 0, stop=k == KH - 1)
                    ins.then_inc(relation_multiplied, 1)
                pe.wait_ge(relation_added, i * R + R)
                pe.matmul(ps_s[G, :], g_eq[G, 0:ET], g_y[G, :], start=True, stop=True).then_inc(sums_made, 1)

        @block.sync
        def _(sp):
            fast_sync(sp)
            with sp.If(uncounted(sp) == 1):
                general_sync(sp)

        @block.gpsimd
        def _(pool):
            fast_pool(pool)
            with pool.If(uncounted(pool) == 1):
                general_pool(pool)

        @block.vector
        def _(dve):
            fast_vector(dve)
            with dve.If(uncounted(dve) == 1):
                general_vector(dve)

        @block.scalar
        def _(act):
            fast_scalar(act)
            with act.If(uncounted(act) == 1):
                general_scalar(act)

        @block.tensor
        def _(pe):
            fast_tensor(pe)
            with pe.If(uncounted(pe) == 1):
                general_tensor(pe)


_INS = ["x", "src", "dst", "edge_type_16", "edge_weight1", "L0_gnn_weight"]


def kernel(**inputs):
    import numpy as np
    import concourse.bacc as bacc
    from concourse.bass_utils import run_bass_kernel_spmd

    nc = bacc.Bacc("TRN2", target_bir_lowering=False, num_devices=1)
    arrays, args = {}, []
    for name in _INS:
        a = np.ascontiguousarray(inputs[name])
        arrays[f"in_{name}"] = a
        args.append(nc.dram_tensor(f"in_{name}", a.shape, mybir.dt.from_np(a.dtype), kind="ExternalInput").ap())
    out = nc.dram_tensor("out", inputs["x"].shape, F32, kind="ExternalOutput").ap()
    build(nc, *args, out)
    return run_bass_kernel_spmd(nc, [arrays], core_ids=[0]).results[0]["out"]
```
